# Optimizing a Trainium2 kernel written in Bass

```python
import numpy as np
import jax
import jax.numpy as jnp

def _softmax(x, axis=-1):
    return jax.nn.softmax(x, axis=axis)

def _gelu(x):
    return jax.nn.gelu(x, approximate=True)

def _silu(x):
    return jax.nn.silu(x)

def _sigmoid(x):
    return jax.nn.sigmoid(x)

def _layernorm(x, axis=-1, eps=1e-05):
    m = jnp.mean(x, axis=axis, keepdims=True)
    v = jnp.var(x, axis=axis, keepdims=True)
    return (x - m) / jnp.sqrt(v + eps)

def _scatter_add(tgt, idx, src, axis=0):
    return tgt.at[idx].add(src)

def _segment_sum(src, seg, n):
    return jax.ops.segment_sum(src, seg, n)
kernel_name = 'mk_xattn_ffn_d1_seqx_r8_80ad2b'

def setup_inputs(seed: int=0):
    np.random.seed(seed)
    _w = jnp.asarray

    def _rec_inputs():
        import jax
        import jax.numpy as jnp
        _rk = jax.random.key(seed)
        x = 7.22e-05 + 1 * jax.random.normal(jax.random.fold_in(_rk, 1), (64, 64, 256), jnp.float32)
        _lenS = 64 - jax.random.randint(jax.random.fold_in(_rk, 7), (64,), 0, max(1, 64 // 4) + 1, jnp.int32)
        _lenS2 = 64 - jax.random.randint(jax.random.fold_in(_rk, 8), (64,), 0, max(1, 64 // 4) + 1, jnp.int32)
        _ctx_1024P = jax.random.normal(jax.random.fold_in(_rk, 11), (64, 16, 128), jnp.float32)
        _ctx_1024c = jax.random.dirichlet(jax.random.fold_in(_rk, 511), 0.3 * jnp.ones((16,), jnp.float32), (64, 64))
        _ctx_1024t = jnp.einsum('bsk,bkd->bsd', _ctx_1024c, _ctx_1024P)
        _ctx_1024t = _ctx_1024t * jax.lax.rsqrt(jnp.mean(jnp.square(_ctx_1024t)) + 1e-12) * 0.953939
        ctx_1024 = -0.000673644 + 1.00013 * (_ctx_1024t + 0.3 * jax.random.normal(jax.random.fold_in(_rk, 611), (64, 64, 128), jnp.float32))
        return (x, ctx_1024)
    x, ctx_1024 = _rec_inputs()

    def _L0_xattn_setup():
        import jax, jax.numpy as jnp
        import numpy as np
        B, S1, S2, DCA = (2, 256, 128, 16)
        QDIM, KDIM, H = (256, 128, 16)
        HD = QDIM // H
        SCALE = HD ** (-0.5)
        EPS = 1e-06
        DCA_WEIGHT = 1.0

        def _ln(t, w, b):
            m = jnp.mean(t, axis=-1, keepdims=True)
            v = jnp.var(t, axis=-1, keepdims=True)
            return (t - m) * jax.lax.rsqrt(v + EPS) * w + b

        def _attn(q, k, v):
            s = jnp.einsum('bhqd,bhkd->bhqk', q, k) * SCALE
            p = jax.nn.softmax(s, axis=-1)
            return jnp.einsum('bhqk,bhkd->bhqd', p, v)
        key = jax.random.key(seed)
        ks = jax.random.split(key, 8)
        w = lambda k, shape: jax.random.normal(k, shape, jnp.float32) * 0.02
        return {'x': jax.random.normal(ks[0], (B, S1, QDIM), jnp.float32), 'y': jax.random.normal(ks[1], (B, S2 + DCA, KDIM), jnp.float32), 'Wq': w(ks[2], (QDIM, QDIM)), 'bq': jnp.zeros((QDIM,), jnp.float32), 'Wk': w(ks[3], (KDIM, QDIM)), 'bk': jnp.zeros((QDIM,), jnp.float32), 'Wv': w(ks[4], (KDIM, QDIM)), 'bv': jnp.zeros((QDIM,), jnp.float32), 'Wkv_dca': w(ks[5], (KDIM, 2 * QDIM)), 'bkv_dca': jnp.zeros((2 * QDIM,), jnp.float32), 'qn_w': jnp.ones((HD,), jnp.float32), 'qn_b': jnp.zeros((HD,), jnp.float32), 'kn_w': jnp.ones((HD,), jnp.float32), 'kn_b': jnp.zeros((HD,), jnp.float32), 'kn_dca_w': jnp.ones((HD,), jnp.float32), 'kn_dca_b': jnp.zeros((HD,), jnp.float32), 'Wo': w(ks[6], (QDIM, QDIM)), 'bo': jnp.zeros((QDIM,), jnp.float32)}
    _L0_xattn_all = _L0_xattn_setup()
    _L0_xattn_in = {k: v for k, v in _L0_xattn_all.items() if k in ('Wq', 'bq', 'Wk', 'bk', 'Wv', 'bv', 'Wkv_dca', 'bkv_dca', 'qn_w', 'qn_b', 'kn_w', 'kn_b', 'kn_dca_w', 'kn_dca_b', 'Wo', 'bo')}
    del _L0_xattn_all

    def _L0_ffn_setup():
        import jax, jax.numpy as jnp
        import numpy as np
        TOP_P = 0.9
        S, B, H, I, E = (256, 4, 256, 512, 8)

        def _top_p_weights(probs, top_p):
            order = jnp.argsort(-probs, axis=-1)
            sp = jnp.take_along_axis(probs, order, axis=-1)
            cum = jnp.cumsum(sp, axis=-1)
            exceed = cum > top_p
            first_idx = jnp.argmax(exceed, axis=-1)
            first = jnp.arange(probs.shape[-1])[None, :] == first_idx[:, None]
            keep = ~exceed | first
            kept = jnp.where(keep, sp, 0.0)
            t_idx = jnp.arange(probs.shape[0])[:, None]
            return jnp.zeros_like(probs).at[t_idx, order].set(kept)
        key = jax.random.key(seed)
        ks = jax.random.split(key, 5)
        scale = 0.02
        return {'hidden_states': jax.random.normal(ks[0], (S, B, H), dtype=jnp.float32), 'router_w': jax.random.normal(ks[1], (E, H), dtype=jnp.float32) * scale, 'gate_w': jax.random.normal(ks[2], (E, I, H), dtype=jnp.float32) * scale, 'up_w': jax.random.normal(ks[3], (E, I, H), dtype=jnp.float32) * scale, 'down_w': jax.random.normal(ks[4], (E, H, I), dtype=jnp.float32) * scale}
    _L0_ffn_all = _L0_ffn_setup()
    _L0_ffn_in = {k: v for k, v in _L0_ffn_all.items() if k in ('router_w', 'gate_w', 'up_w', 'down_w')}
    del _L0_ffn_all
    return {'x': x, 'ctx_1024': ctx_1024, 'L0_xattn_Wq': _L0_xattn_in['Wq'], 'L0_xattn_bq': _L0_xattn_in['bq'], 'L0_xattn_Wk': _L0_xattn_in['Wk'], 'L0_xattn_bk': _L0_xattn_in['bk'], 'L0_xattn_Wv': _L0_xattn_in['Wv'], 'L0_xattn_bv': _L0_xattn_in['bv'], 'L0_xattn_Wkv_dca': _L0_xattn_in['Wkv_dca'], 'L0_xattn_bkv_dca': _L0_xattn_in['bkv_dca'], 'L0_xattn_qn_w': _L0_xattn_in['qn_w'], 'L0_xattn_qn_b': _L0_xattn_in['qn_b'], 'L0_xattn_kn_w': _L0_xattn_in['kn_w'], 'L0_xattn_kn_b': _L0_xattn_in['kn_b'], 'L0_xattn_kn_dca_w': _L0_xattn_in['kn_dca_w'], 'L0_xattn_kn_dca_b': _L0_xattn_in['kn_dca_b'], 'L0_xattn_Wo': _L0_xattn_in['Wo'], 'L0_xattn_bo': _L0_xattn_in['bo'], 'L0_ffn_router_w': _L0_ffn_in['router_w'], 'L0_ffn_gate_w': _L0_ffn_in['gate_w'], 'L0_ffn_up_w': _L0_ffn_in['up_w'], 'L0_ffn_down_w': _L0_ffn_in['down_w']}

def reference(x, ctx_1024, L0_xattn_Wq, L0_xattn_bq, L0_xattn_Wk, L0_xattn_bk, L0_xattn_Wv, L0_xattn_bv, L0_xattn_Wkv_dca, L0_xattn_bkv_dca, L0_xattn_qn_w, L0_xattn_qn_b, L0_xattn_kn_w, L0_xattn_kn_b, L0_xattn_kn_dca_w, L0_xattn_kn_dca_b, L0_xattn_Wo, L0_xattn_bo, L0_ffn_router_w, L0_ffn_gate_w, L0_ffn_up_w, L0_ffn_down_w):
    import jax
    import jax.numpy as jnp

    def _L0_xattn_ref(x, y, Wq, bq, Wk, bk, Wv, bv, Wkv_dca, bkv_dca, qn_w, qn_b, kn_w, kn_b, kn_dca_w, kn_dca_b, Wo, bo):
        import jax, jax.numpy as jnp
        import numpy as np
        B, S1, S2, DCA = (2, 256, 128, 16)
        QDIM, KDIM, H = (256, 128, 16)
        HD = QDIM // H
        SCALE = HD ** (-0.5)
        EPS = 1e-06
        DCA_WEIGHT = 1.0

        def _ln(t, w, b):
            m = jnp.mean(t, axis=-1, keepdims=True)
            v = jnp.var(t, axis=-1, keepdims=True)
            return (t - m) * jax.lax.rsqrt(v + EPS) * w + b

        def _attn(q, k, v):
            s = jnp.einsum('bhqd,bhkd->bhqk', q, k) * SCALE
            p = jax.nn.softmax(s, axis=-1)
            return jnp.einsum('bhqk,bhkd->bhqd', p, v)
        b, s1, _ = x.shape
        y_dca = y[:, -DCA:, :]
        y_main = y[:, :-DCA, :]
        kv_dca = (y_dca @ Wkv_dca + bkv_dca).reshape(b, DCA, 2, H, HD)
        k_dca = _ln(kv_dca[:, :, 0], kn_dca_w, kn_dca_b)
        v_dca = kv_dca[:, :, 1]
        s2 = y_main.shape[1]
        q = _ln((x @ Wq + bq).reshape(b, s1, H, HD), qn_w, qn_b)
        kv = jnp.concatenate([y_main @ Wk + bk, y_main @ Wv + bv], axis=-1)
        kv = kv.reshape(b, s2, H, 2 * HD)
        k = _ln(kv[..., :HD], kn_w, kn_b)
        v = kv[..., HD:]
        qT = q.transpose(0, 2, 1, 3)
        ctx = _attn(qT, k.transpose(0, 2, 1, 3), v.transpose(0, 2, 1, 3))
        ctx = ctx.transpose(0, 2, 1, 3).reshape(b, s1, QDIM)
        ctx_dca = _attn(qT, k_dca.transpose(0, 2, 1, 3), v_dca.transpose(0, 2, 1, 3))
        ctx_dca = ctx_dca.transpose(0, 2, 1, 3).reshape(b, s1, QDIM)
        ctx = ctx + DCA_WEIGHT * ctx_dca
        return ctx @ Wo + bo

    def _L0_ffn_ref(hidden_states, router_w, gate_w, up_w, down_w):
        import jax, jax.numpy as jnp
        import numpy as np
        TOP_P = 0.9
        S, B, H, I, E = (256, 4, 256, 512, 8)

        def _top_p_weights(probs, top_p):
            order = jnp.argsort(-probs, axis=-1)
            sp = jnp.take_along_axis(probs, order, axis=-1)
            cum = jnp.cumsum(sp, axis=-1)
            exceed = cum > top_p
            first_idx = jnp.argmax(exceed, axis=-1)
            first = jnp.arange(probs.shape[-1])[None, :] == first_idx[:, None]
            keep = ~exceed | first
            kept = jnp.where(keep, sp, 0.0)
            t_idx = jnp.arange(probs.shape[0])[:, None]
            return jnp.zeros_like(probs).at[t_idx, order].set(kept)
        s, b, h = hidden_states.shape
        x = hidden_states.reshape(-1, h)
        probs = jax.nn.softmax(x @ router_w.T, axis=-1)
        w = _top_p_weights(probs, TOP_P)
        out = jnp.zeros_like(x)
        n_exp = router_w.shape[0]
        for e in range(n_exp):
            g = jax.nn.silu(x @ gate_w[e].T)
            u = x @ up_w[e].T
            y = g * u @ down_w[e].T
            out = out + y * w[:, e:e + 1]
        return out.reshape(s, b, h)
    x = x + _L0_xattn_ref(_layernorm(x, axis=-1), ctx_1024, L0_xattn_Wq, L0_xattn_bq, L0_xattn_Wk, L0_xattn_bk, L0_xattn_Wv, L0_xattn_bv, L0_xattn_Wkv_dca, L0_xattn_bkv_dca, L0_xattn_qn_w, L0_xattn_qn_b, L0_xattn_kn_w, L0_xattn_kn_b, L0_xattn_kn_dca_w, L0_xattn_kn_dca_b, L0_xattn_Wo, L0_xattn_bo)
    x = x + _L0_ffn_ref(_layernorm(x, axis=-1), L0_ffn_router_w, L0_ffn_gate_w, L0_ffn_up_w, L0_ffn_down_w)
    return x

_drawn_inputs = setup_inputs


def setup_inputs(seed=0):
    import zlib

    import numpy as np

    out = dict(_drawn_inputs(seed))
    spreads = {'L0_xattn_bq': (0.0, 0.8),
     'L0_xattn_bk': (0.0, 0.401),
     'L0_xattn_bv': (0.0, 0.331),
     'L0_xattn_bkv_dca': (0.0, 0.1),
     'L0_xattn_qn_w': (1.0, 0.6),
     'L0_xattn_qn_b': (0.0, 0.8),
     'L0_xattn_kn_w': (1.0, 0.6),
     'L0_xattn_kn_b': (0.0, 0.8),
     'L0_xattn_kn_dca_w': (1.0, 0.6),
     'L0_xattn_kn_dca_b': (0.0, 0.8),
     'L0_xattn_bo': (0.0, 0.1)}
    factors = {'L0_ffn_router_w': 8.0,
     'L0_ffn_gate_w': 6.593,
     'L0_ffn_up_w': 6.507,
     'L0_ffn_down_w': 6.518}
    for name, (base, spread) in spreads.items():
        noise = np.random.default_rng([zlib.crc32(name.encode()), seed]).standard_normal(out[name].shape)
        drawn = base * np.exp(spread * noise) if base else spread * noise
        out[name] = jnp.asarray(drawn.astype(out[name].dtype))
    for name, factor in factors.items():
        out[name] = (out[name] * factor).astype(out[name].dtype)
    return out
```

```python
import concourse.bass as bass
from concourse import mybir
from contextlib import ExitStack

BATCH, SEQ, D = 64, 64, 256
KEYS, KEYS_MAIN, CD = 64, 48, 128
HEADS, HD = 16, 16
EXPERTS, INNER = 8, 512
TOP_P = 0.9
P = 128
TOKENS = BATCH * SEQ
TILES = TOKENS // P
BPT = P // SEQ
KD = D // P
HG = P // HD
PAIRS = HEADS // 2
BLOCK = 512
BLOCKS = TOKENS // BLOCK
HI_LO = [[1, 0], [1, 0], [0, 1], [0, 1]]
TPB = BLOCK // P
MT = INNER // P
WPART = KD * INNER


def xattn_ffn_kernel(nc, x, ctx_t, wq, wkv_main, wkv_dca, wo, router, w_ffn, ln_scales,
                     q_bias, k_bias, o_bias, v_bias, ident, head_mask, pair_mask, row_mask,
                     hi_lo_rows, before, out):
    f32, f32r = mybir.dt.float32, mybir.dt.float32r
    ALU, ACT, AX = mybir.AluOpType, mybir.ActivationFunctionType, mybir.AxisListType
    dve, act_e, pool_e, te = nc.vector, nc.scalar, nc.gpsimd, nc.tensor

    whole = ExitStack()
    with whole:
        def sem(name):
            return whole.enter_context(nc.semaphore(name))

        def keep(name, shape, dt=f32):
            return whole.enter_context(nc.sbuf_tensor(name, shape, dt))

        acc = keep("acc", [P, TILES, D])
        xt_hi = keep("xt_hi", [P, KD, TOKENS], f32r)
        xt_lo = keep("xt_lo", [P, KD, TOKENS], f32r)
        logits = keep("logits", [P, TILES, EXPERTS])
        weights = keep("weights", [P, TILES, EXPERTS])
        before_s = keep("before_s", [P, EXPERTS, EXPERTS])

        phase = ExitStack()

        def sb(name, shape, dt=f32):
            return phase.enter_context(nc.sbuf_tensor(name, shape, dt))

        ident_s = sb("ident_s", [P, P])
        wq_s = sb("wq_s", [P, KD, D])
        wkm_s = sb("wkm_s", [P, 2 * D])
        wkd_s = sb("wkd_s", [P, 2 * D])
        wo_s = sb("wo_s", [P, KD, D])
        rt_s = sb("rt_s", [P, KD, EXPERTS])
        lnp = sb("lnp", [P, 6])
        vb_s = sb("vb_s", [P, 2, KD])
        vb_sum = sb("vb_sum", [P, KD])
        hmask = sb("hmask", [P, HG])
        pmask = sb("pmask", [P, D])
        rmask_f = sb("rmask_f", [4, P])
        rmask = sb("rmask", [4, P], f32r)
        hilo = sb("hilo", [4, 2])
        bias_f = sb("bias_f", [4, 3, D])
        bias_t = sb("bias_t", [4, 3, D])
        bias_h = sb("bias_h", [4, 3, D], f32r)
        bias_u = sb("bias_u", [4, 3, D])
        bias_r = sb("bias_r", [4, 3, D], f32r)
        gsum = sb("gsum", [P, 4, HEADS])
        gsum_b = sb("gsum_b", [4, 2, HEADS])
        minus_half = sb("minus_half", [P, 2 * HEADS])
        eps_model = sb("eps_model", [P, 1])
        eps_heads = sb("eps_heads", [P, 2 * HEADS])
        hold = sb("hold", [P, 1])

        cm = [sb(f"cm{p}", [P, BPT * 2, KEYS]) for p in (0, 1)]
        cd = [sb(f"cd{p}", [P, BPT * 2, KEYS]) for p in (0, 1)]
        st1, st2 = sb("st1", [P, 6]), sb("st2", [P, 6])
        mv1 = [sb(f"mv1{p}", [P, 2]) for p in (0, 1)]
        mv2 = [sb(f"mv2{p}", [P, 2]) for p in (0, 1)]
        rs1 = [sb(f"rs1{p}", [P, 2]) for p in (0, 1)]
        rs2 = [sb(f"rs2{p}", [P, 2]) for p in (0, 1)]
        xn = [sb(f"xn{p}", [P, D]) for p in (0, 1)]
        xnt = [sb(f"xnt{p}", [P, KD, P]) for p in (0, 1)]
        sq = [sb(f"sq{p}", [P, 2 * D]) for p in (0, 1)]
        ss = [sb(f"ss{p}", [P, 2 * HEADS]) for p in (0, 1)]
        rsq = [sb(f"rsq{p}", [P, 2, 2 * HEADS]) for p in (0, 1)]
        qkn = [sb(f"qkn{p}", [P, 2 * D]) for p in (0, 1)]
        vbd = [sb(f"vbd{p}", [P, BPT, D]) for p in (0, 1)]
        qt = [sb(f"qt{p}", [P, KD, P]) for p in (0, 1)]
        kt = [sb(f"kt{p}", [P, KD, BPT, KEYS]) for p in (0, 1)]
        kbd = [sb(f"kbd{p}", [P, BPT, KD, HG, KEYS]) for p in (0, 1)]
        mx = sb("mx", [P, 2, HEADS])
        sm = [sb(f"sm{p}", [P, 2, HEADS]) for p in (0, 1)]
        rc = [sb(f"rc{p}", [P, 2, HEADS]) for p in (0, 1)]
        pr = [sb(f"pr{p}", [P, HEADS, KEYS]) for p in (0, 1)]
        pt = [sb(f"pt{p}", [P, PAIRS, P]) for p in (0, 1)]
        ctxt = [sb(f"ctxt{p}", [P, KD, P]) for p in (0, 1)]
        x1n = [sb(f"x1n{p}", [P, D]) for p in (0, 1)]
        x1nt = [sb(f"x1nt{p}", [P, KD, P]) for p in (0, 1)]
        phase.close()

        phase = ExitStack()
        w_raw = sb("w_raw", [P, 3 * WPART])
        w_hi = [sb(f"w_hi{p}", [P, 3 * WPART], f32r) for p in (0, 1)]
        w_lo = [sb(f"w_lo{p}", [P, 3 * WPART], f32r) for p in (0, 1)]
        h_hi = [sb(f"h_hi{p}", [P, MT, BLOCK], f32r) for p in (0, 1)]
        h_lo = [sb(f"h_lo{p}", [P, MT, BLOCK], f32r) for p in (0, 1)]
        th = [sb(f"th{p}", [P, BLOCK]) for p in (0, 1)]
        sg = [sb(f"sg{p}", [P, BLOCK]) for p in (0, 1)]
        hf = [sb(f"hf{p}", [P, BLOCK]) for p in (0, 1)]
        phase.close()
        phase = ExitStack()
        lmax = sb("lmax", [P, TILES])
        lex = sb("lex", [P, TILES, EXPERTS])
        lsum = sb("lsum", [P, TILES])
        lrec = sb("lrec", [P, TILES])
        prob = sb("prob", [P, TILES, EXPERTS])
        gt = sb("gt", [P, TILES, EXPERTS, EXPERTS])
        eq = sb("eq", [P, TILES, EXPERTS, EXPERTS])
        cum = sb("cum", [P, TILES, EXPERTS])
        phase.close()

        def bank(stack, name, n=1):
            return stack.enter_context(nc.psum_tensor(name, [P, n, 512], f32))

        ps = ExitStack()
        b_qk = bank(ps, "b_qk")
        b_v = bank(ps, "b_v")
        b_x = bank(ps, "b_x")
        b_qkt = bank(ps, "b_qkt")
        b_s = bank(ps, "b_s", 2)
        b_pt = bank(ps, "b_pt")
        b_c = bank(ps, "b_c")
        ps.close()
        ps = ExitStack()
        b_gate = [bank(ps, f"b_gate{p}") for p in (0, 1)]
        b_up = [bank(ps, f"b_up{p}") for p in (0, 1)]
        b_down = [bank(ps, f"b_down{p}") for p in (0, 1)]
        ps.close()

        const_in, x_in = sem("const_in"), sem("x_in")
        zeroed = sem("zeroed")
        prep = sem("prep")
        ctx_in = [sem("ctx_in0"), sem("ctx_in1")]
        st1_done, mv1_done, rs1a_done, rs1_done = sem("st1_done"), sem("mv1_done"), sem("rs1a_done"), sem("rs1_done")
        xn_done, xnt_ps, xnt_done = sem("xn_done"), sem("xnt_ps"), sem("xnt_done")
        v_ps, qk_ps, sq_done, ss_done = sem("v_ps"), sem("qk_ps"), sem("sq_done"), sem("ss_done")
        rsqa_done, rsq_done, qkn_done, vbd_done = sem("rsqa_done"), sem("rsq_done"), sem("qkn_done"), sem("vbd_done")
        qkt_ps, qkt_done, kbd_done = sem("qkt_ps"), sem("qkt_done"), sem("kbd_done")
        s_ps, mx_done, sub_done, exp_done = sem("s_ps"), sem("mx_done"), sem("sub_done"), sem("exp_done")
        sm_done, rc_done, pn_done = sem("sm_done"), sem("rc_done"), sem("pn_done")
        pt_ps, pt_done, c_ps, ctxt_done = sem("pt_ps"), sem("pt_done"), sem("c_ps"), sem("ctxt_done")
        o_ps, x1_done, st2_done, mv2_done = sem("o_ps"), sem("x1_done"), sem("st2_done"), sem("mv2_done")
        rs2a_done, rs2_done, x1n_done = sem("rs2a_done"), sem("rs2_done"), sem("x1n_done")
        x1nt_ps, x1nt_done, lg_ps, lg_done = sem("x1nt_ps"), sem("x1nt_done"), sem("lg_ps"), sem("lg_done")
        hi_done, lo_done = sem("hi_done"), sem("lo_done")
        route, route_exp = sem("route"), sem("route_exp")
        w_in, w_hi_done, w_lo_done = sem("w_in"), sem("w_hi_done"), sem("w_lo_done")
        gate_ps, up_ps, tanh_done = sem("gate_ps"), sem("up_ps"), sem("tanh_done")
        sg_done, hf_done, h_hi_done, h_lo_done = sem("sg_done"), sem("hf_done"), sem("h_hi_done"), sem("h_lo_done")
        down_ps, acc_half, acc_done, stored = sem("down_ps"), sem("acc_half"), sem("acc_done"), sem("stored")

        ROUTE_STEPS = 14
        PREP_ALL = 16

        class Tile:
            def __init__(self, i, parity):
                self.i, self.par = i, parity
                self.t = 2 * i + parity

            def back(self, k):
                par = (self.par - k) % 2
                return Tile(self.i + (self.par - k - par) // 2, par)

        def before_tile(eng, s, t, per=1, ago=2, extra=0):
            if isinstance(t, int) and t - ago < 0:
                return
            eng.wait_ge(s, (t - ago + 1) * per + extra)

        def run_tiles(eng, body):
            body(Tile(0, 0), [0])
            body(Tile(0, 1), [0, 1])
            for par in (0, 1):
                body(Tile(1, par), [0, 1, 2])
            with eng.Fori(2, TILES // 2) as i:
                for par in (0, 1):
                    body(Tile(i, par), [0, 1, 2])
            body(Tile(TILES // 2, 0), [1, 2])
            body(Tile(TILES // 2, 1), [2])

        block = whole.enter_context(nc.Block())

        @block.sync
        def _(sp):
            for dst, src in ((ident_s[:], ident), (wq_s[:], wq), (wkm_s[:], wkv_main), (wkd_s[:], wkv_dca),
                             (wo_s[:], wo), (rt_s[:], router), (lnp[:], ln_scales), (vb_s[:], v_bias),
                             (hmask[:], head_mask), (pmask[:], pair_mask), (rmask_f[:], row_mask),
                             (hilo[:], hi_lo_rows), (before_s[:], before), (bias_f[:, 0, :], q_bias),
                             (bias_f[:, 1, :], k_bias), (bias_f[:, 2, :], o_bias)):
                sp.dma_start(dst, src).then_inc(const_in, 16)
            for t8 in range(4):
                n = TILES // 4
                sp.dma_start(acc[:, t8 * n:(t8 + 1) * n, :],
                             x[t8 * n * P:(t8 + 1) * n * P, :].rearrange("(t p) d -> p t d", p=P)).then_inc(x_in, 16)
            sp.wait_ge(zeroed, 1)

            def load_ctx(tile):
                before_tile(sp, v_ps, tile.t)
                b0 = tile.t * (BPT * KEYS)
                src = ctx_t[:, bass.ds(b0, BPT * KEYS)].rearrange("p (b k) -> p b k", k=KEYS)
                for buf, lo, hi in ((cm[tile.par], 0, KEYS_MAIN), (cd[tile.par], KEYS_MAIN, KEYS)):
                    for copy in range(2):
                        sp.dma_start(buf[:].rearrange("p (b c) k -> p b c k", c=2)[:, :, copy, lo:hi],
                                     src[:, :, lo:hi]).then_inc(ctx_in[tile.par], 16)

            load_ctx(Tile(0, 0))
            load_ctx(Tile(0, 1))
            with sp.Fori(1, TILES // 2) as i:
                load_ctx(Tile(i, 0))
                load_ctx(Tile(i, 1))

            sp.wait_ge(lo_done, TILES)
            sp.wait_ge(x1nt_ps, TILES)
            sp.wait_ge(lg_done, TILES)
            sp.wait_ge(route, ROUTE_STEPS)
            for e in range(EXPERTS):
                if e:
                    sp.wait_ge(w_lo_done, 3 * e)
                sp.dma_start(w_raw[:], w_ffn[e]).then_inc(w_in, 16)
            sp.wait_ge(acc_done, EXPERTS * BLOCKS)
            sp.dma_start(out.rearrange("(t p) d -> p t d", p=P), acc[:]).then_inc(stored, 16)
            sp.wait_ge(stored, 16)



        @block.gpsimd
        def _(pool):
            for n, b in enumerate(cm + cd):
                nc.gpsimd.memset(b[:], 0.0)
            nc.gpsimd.memset(eps_model[:], 1e-5)
            nc.gpsimd.memset(eps_heads[:], 1e-6 * HD)
            nc.gpsimd.memset(minus_half[:], -0.5).then_inc(zeroed, 1)
            pool.wait_ge(zeroed, 1)
            pool.wait_ge(const_in, 16 * 16)

            def body(tile, stages):
                t, p = tile.t, tile.par
                if 1 in stages:
                    a = tile.back(1)
                    pool.wait_ge(qkt_done, a.t + 1)
                    before_tile(pool, s_ps, a.t)
                    for b in range(BPT):
                        l = nc.gpsimd.tensor_tensor(
                            kbd[a.par][:, b], kt[a.par][:, :, b, :].unsqueeze(2).broadcast_to([P, KD, HG, KEYS]),
                            hmask[:].unsqueeze(1).unsqueeze(3).broadcast_to([P, KD, HG, KEYS]), ALU.mult)
                    l.then_inc(kbd_done, 1)
                if 0 in stages:
                    pool.wait_ge(mv1_done, t + 1)
                    before_tile(pool, xn_done, t)
                    nc.gpsimd.tensor_tensor(rs1[p][:, 0:1], mv1[p][:, 1:2], eps_model[:], ALU.add).then_inc(rs1a_done, 1)
                    pool.wait_ge(rs1a_done, t + 1)
                    nc.gpsimd.tensor_tensor(rs1[p][:, 1:2], rs1[p][:, 0:1], minus_half[:, 0:1], ALU.pow).then_inc(rs1_done, 1)
                if 2 in stages:
                    c = tile.back(2)
                    q = c.par
                    pool.wait_ge(rc_done, c.t + 1)
                    nc.gpsimd.tensor_tensor(pr[q][:, :, 0:KEYS_MAIN], pr[q][:, :, 0:KEYS_MAIN],
                                            rc[q][:, 0, :].unsqueeze(2).broadcast_to([P, HEADS, KEYS_MAIN]), ALU.mult)
                    nc.gpsimd.tensor_tensor(pr[q][:, :, KEYS_MAIN:KEYS], pr[q][:, :, KEYS_MAIN:KEYS],
                                            rc[q][:, 1, :].unsqueeze(2).broadcast_to([P, HEADS, KEYS - KEYS_MAIN]),
                                            ALU.mult).then_inc(pn_done, 1)
                if 0 in stages:
                    pool.wait_ge(ss_done, t + 1)
                    before_tile(pool, qkn_done, t)
                    nc.gpsimd.tensor_tensor(rsq[p][:, 0, :], ss[p][:], eps_heads[:], ALU.add).then_inc(rsqa_done, 1)
                    pool.wait_ge(rsqa_done, t + 1)
                    nc.gpsimd.tensor_tensor(rsq[p][:, 1, :], rsq[p][:, 0, :], minus_half[:], ALU.pow).then_inc(rsq_done, 1)
                if 2 in stages:
                    pool.wait_ge(mv2_done, c.t + 1)
                    before_tile(pool, x1n_done, c.t)
                    nc.gpsimd.tensor_tensor(rs2[q][:, 0:1], mv2[q][:, 1:2], eps_model[:], ALU.add).then_inc(rs2a_done, 1)
                    pool.wait_ge(rs2a_done, c.t + 1)
                    nc.gpsimd.tensor_tensor(rs2[q][:, 1:2], rs2[q][:, 0:1], minus_half[:, 0:1], ALU.pow).then_inc(rs2_done, 1)

            run_tiles(pool, body)

            def split_weights(e):
                pool.wait_ge(w_in, 16 * (e + 1))
                for part in range(3):
                    pool.wait_ge(w_hi_done, 3 * e + part + 1)
                    if isinstance(e, int) and e >= 2 or not isinstance(e, int):
                        pool.wait_ge(down_ps, 2 * BLOCKS * (e - 1))
                    s = slice(part * WPART, (part + 1) * WPART)
                    nc.gpsimd.tensor_tensor(w_lo[e % 2][:, s], w_raw[:, s], w_hi[e % 2][:, s].bitcast(f32),
                                            ALU.subtract).then_inc(w_lo_done, 1)

            def rest(step, par):
                for m in range(MT):
                    n = step * MT + m
                    pool.wait_ge(h_hi_done, n + 1)
                    if not (isinstance(step, int) and step < 2):
                        pool.wait_ge(down_ps, 2 * (step - 1))
                    nc.gpsimd.tensor_tensor(h_lo[par][:, m, :], hf[m % 2][:], h_hi[par][:, m, :].bitcast(f32),
                                            ALU.subtract).then_inc(h_lo_done, 1)

            split_weights(0)
            for e in range(EXPERTS):
                rest(e * BLOCKS, 0)
                if e + 1 < EXPERTS:
                    pass
                rest(e * BLOCKS + 1, 1)
                if e + 1 < EXPERTS:
                    split_weights(e + 1)
                with pool.Fori(1, BLOCKS // 2) as j:
                    rest(2 * j + e * BLOCKS, 0)
                    rest(2 * j + (e * BLOCKS + 1), 1)

        @block.scalar
        def _(act):
            act.wait_ge(prep, PREP_ALL)

            def body(tile, stages):
                t, p = tile.t, tile.par
                if 1 in stages:
                    a = tile.back(1)
                    act.wait_ge(sub_done, a.t + 1)
                    nc.scalar.activation(pr[a.par][:], pr[a.par][:], ACT.Exp, scale=HD ** -0.5).then_inc(exp_done, 1)
                if 0 in stages:
                    act.wait_ge(xnt_ps, t + 1)
                    before_tile(act, qk_ps, t)
                    nc.scalar.copy(xnt[p][:], b_x[:, 0, 0:D].rearrange("p (k n) -> p k n", k=KD)).then_inc(xnt_done, 1)
                if 2 in stages:
                    c = tile.back(2)
                    q = c.par
                    for half in range(2):
                        act.wait_ge(pt_ps, 2 * c.t + half + 1)
                        before_tile(act, c_ps, c.t)
                        hp = PAIRS // 2
                        nc.scalar.copy(pt[q][:, half * hp:(half + 1) * hp, :],
                                       b_pt[:, 0, :].rearrange("p (j n) -> p j n", j=hp)).then_inc(pt_done, 1)
                if 0 in stages:
                    act.wait_ge(qk_ps, t + 1)
                    before_tile(act, ss_done, t)
                    nc.scalar.activation(sq[p][:], b_qk[:, 0, :], ACT.Square).then_inc(sq_done, 1)
                if 2 in stages:
                    act.wait_ge(c_ps, c.t + 1)
                    before_tile(act, o_ps, c.t)
                    for g in range(KD):
                        nc.scalar.activation(ctxt[q][:, g, :], b_c[:, 0, g * P:(g + 1) * P], ACT.Identity,
                                             bias=vb_sum[:, g:g + 1]).then_inc(ctxt_done, 1)
                if 0 in stages:
                    act.wait_ge(qkt_ps, t + 1)
                    before_tile(act, s_ps, t)
                    before_tile(act, kbd_done, t)
                    w = b_qkt[:, 0, :].rearrange("p (a k b n) -> p a k b n", a=2, k=KD, b=BPT)
                    nc.scalar.activation(qt[p][:], b_qkt[:, 0, 0:D].rearrange("p (k n) -> p k n", k=KD), ACT.Identity,
                                         bias=lnp[:, 1:2], scale=lnp[:, 0:1])
                    nc.scalar.activation(kt[p][:, :, :, 0:KEYS_MAIN], w[:, 1, :, :, 0:KEYS_MAIN], ACT.Identity,
                                         bias=lnp[:, 3:4], scale=lnp[:, 2:3])
                    nc.scalar.activation(kt[p][:, :, :, KEYS_MAIN:KEYS], w[:, 1, :, :, KEYS_MAIN:KEYS], ACT.Identity,
                                         bias=lnp[:, 5:6], scale=lnp[:, 4:5]).then_inc(qkt_done, 1)
                if 2 in stages:
                    act.wait_ge(x1nt_ps, c.t + 1)
                    before_tile(act, lg_ps, c.t)
                    before_tile(act, lo_done, c.t)
                    nc.scalar.copy(x1nt[q][:], b_x[:, 0, D:2 * D].rearrange("p (k n) -> p k n", k=KD)).then_inc(x1nt_done, 1)
                    act.wait_ge(lg_ps, c.t + 1)
                    nc.scalar.copy(logits[:, bass.ds(c.t, 1), :], b_c[:, :, 0:EXPERTS]).then_inc(lg_done, 1)

            run_tiles(act, body)

            act.wait_ge(route, 2)
            nc.scalar.activation(lex[:], lex[:], ACT.Exp).then_inc(route_exp, 1)

            def split_weights(e):
                act.wait_ge(w_in, 16 * (e + 1))
                if e >= 2:
                    act.wait_ge(down_ps, 2 * BLOCKS * (e - 1))
                if e:
                    act.wait_ge(w_lo_done, 3 * e)
                for part in range(3):
                    s = slice(part * WPART, (part + 1) * WPART)
                    nc.scalar.copy(w_hi[e % 2][:, s], w_raw[:, s]).then_inc(w_hi_done, 1)

            def inner(step, par):
                for m in range(MT):
                    n = step * MT + m
                    act.wait_ge(gate_ps, n + 1)
                    if not (isinstance(n, int) and n < 2):
                        act.wait_ge(sg_done, n - 1)
                    nc.scalar.activation(th[m % 2][:], b_gate[m % 2][:, 0, :], ACT.Tanh, scale=0.5).then_inc(tanh_done, 1)
                    if m:
                        leading(n - 1, step, par, m - 1)
                leading(step * MT + MT - 1, step, par, MT - 1)

            def leading(n, step, par, m):
                act.wait_ge(hf_done, n + 1)
                if not (isinstance(step, int) and step < 2):
                    act.wait_ge(down_ps, 2 * (step - 1))
                nc.scalar.copy(h_hi[par][:, m, :], hf[m % 2][:]).then_inc(h_hi_done, 1)

            split_weights(0)
            for e in range(EXPERTS):
                inner(e * BLOCKS, 0)
                inner(e * BLOCKS + 1, 1)
                if e + 1 < EXPERTS:
                    split_weights(e + 1)
                with act.Fori(1, BLOCKS // 2) as j:
                    inner(2 * j + e * BLOCKS, 0)
                    inner(2 * j + (e * BLOCKS + 1), 1)

        @block.vector
        def _(ve):
            step = [0]

            def chained(ins):
                step[0] += 1
                ins.then_inc(prep, 1)
                ve.wait_ge(prep, step[0])

            ve.wait_ge(const_in, 16 * 16)
            chained(dve.tensor_reduce(gsum[:, 0:2, :], wq_s[:].rearrange("p k (h d) -> p k h d", d=HD), AX.X, ALU.add))
            chained(dve.tensor_reduce(gsum[:, 2, :], wkm_s[:, 0:D].rearrange("p (h d) -> p h d", d=HD), AX.X, ALU.add))
            chained(dve.tensor_reduce(gsum[:, 3, :], wkd_s[:, 0:D].rearrange("p (h d) -> p h d", d=HD), AX.X, ALU.add))
            chained(dve.tensor_scalar(gsum[:], gsum[:], 1.0 / HD, None, ALU.mult))

            def center(w, mean):
                v = w.rearrange("p (h d) -> p h d", d=HD)
                return dve.tensor_tensor(v, v, mean.unsqueeze(2).broadcast_to([v.shape[0], HEADS, HD]), ALU.subtract)

            for k in range(KD):
                center(wq_s[:, k, :], gsum[:, k, :])
            center(wkm_s[:, 0:D], gsum[:, 2, :])
            chained(center(wkd_s[:, 0:D], gsum[:, 3, :]))
            chained(dve.tensor_reduce(gsum_b[:], bias_f[:, 0:2, :].rearrange("p k (h d) -> p k h d", d=HD), AX.X, ALU.add))
            chained(dve.tensor_scalar(gsum_b[:], gsum_b[:], 1.0 / HD, None, ALU.mult))
            center(bias_f[:, 0, :], gsum_b[:, 0, :])
            chained(center(bias_f[:, 1, :], gsum_b[:, 1, :]))
            chained(dve.tensor_copy(bias_h[:], bias_f[:]))
            chained(dve.tensor_tensor(bias_t[:], bias_f[:], bias_h[:].bitcast(f32), ALU.subtract))
            chained(dve.tensor_scalar(bias_u[:], bias_h[:].bitcast(f32), hilo[:, 0:1], None, ALU.mult))
            chained(dve.tensor_scalar(bias_t[:], bias_t[:], hilo[:, 1:2], None, ALU.mult))
            chained(dve.tensor_tensor(bias_r[:], bias_u[:], bias_t[:], ALU.add))
            chained(dve.tensor_copy(rmask[:], rmask_f[:]))
            chained(dve.tensor_scalar(lnp[:, 0:6:2], lnp[:, 0:6:2], HD ** 0.5, None, ALU.mult))
            chained(dve.tensor_tensor(vb_sum[:], vb_s[:, 0, :], vb_s[:, 1, :], ALU.add))
            assert step[0] == PREP_ALL, step[0]
            ve.wait_ge(x_in, 4 * 16)

            def held(ve):
                dve.memset(hold[:], 0.0)

            def body(tile, stages):
                t, p = tile.t, tile.par
                if 1 in stages:
                    a = tile.back(1)
                    ap = a.par
                    sc = b_s[:].rearrange("p g (h k) -> p (g h) k", k=KEYS)
                    parts = ((0, 0, KEYS_MAIN), (1, KEYS_MAIN, KEYS))
                    ve.wait_ge(s_ps, a.t + 1)
                    before_tile(ve, pt_ps, a.t, per=2)
                    for n, lo, hi in parts:
                        l = dve.tensor_reduce(mx[:, n, :], sc[:, :, lo:hi], AX.X, ALU.max)
                    l.then_inc(mx_done, 1)
                    ve.wait_ge(mx_done, a.t + 1)
                    for n, lo, hi in parts:
                        l = dve.tensor_tensor(pr[ap][:, :, lo:hi], sc[:, :, lo:hi],
                                              mx[:, n, :].unsqueeze(2).broadcast_to([P, HEADS, hi - lo]), ALU.subtract)
                    l.then_inc(sub_done, 1)
                if 0 in stages:
                    held(ve)
                    dve.bn_stats(st1[:], acc[:, bass.ds(t, 1), :]).then_inc(st1_done, 1)
                    ve.wait_ge(st1_done, t + 1)
                    before_tile(ve, rs1_done, t)
                    held(ve)
                    dve.bn_aggr(mv1[p][:], st1[:]).then_inc(mv1_done, 1)
                    ve.wait_ge(mv1_done, t + 1)
                    ve.wait_ge(rs1_done, t + 1)
                    before_tile(ve, xnt_ps, t)
                    dve.tensor_scalar(xn[p][:], acc[:, bass.ds(t, 1), :].rearrange("p o d -> p (o d)"),
                                      mv1[p][:, 0:1], rs1[p][:, 1:2], ALU.subtract, ALU.mult).then_inc(xn_done, 1)
                if 1 in stages:
                    ve.wait_ge(v_ps, a.t + 1)
                    before_tile(ve, c_ps, a.t)
                    dve.tensor_tensor(vbd[ap][:], b_v[:, 0, :].rearrange("p (b d) -> p b d", b=BPT),
                                      pmask[:].unsqueeze(1).broadcast_to([P, BPT, D]), ALU.mult).then_inc(vbd_done, 1)
                    ve.wait_ge(exp_done, a.t + 1)
                    for n, lo, hi in parts:
                        l = dve.tensor_reduce(sm[ap][:, n, :], pr[ap][:, :, lo:hi], AX.X, ALU.add)
                    l.then_inc(sm_done, 1)
                    ve.wait_ge(sm_done, a.t + 1)
                    before_tile(ve, pn_done, a.t)
                    dve.reciprocal(rc[ap][:], sm[ap][:]).then_inc(rc_done, 1)
                if 0 in stages:
                    ve.wait_ge(sq_done, t + 1)
                    before_tile(ve, rsqa_done, t)
                    dve.tensor_reduce(ss[p][:], sq[p][:].rearrange("p (h d) -> p h d", d=HD), AX.X, ALU.add).then_inc(ss_done, 1)
                    ve.wait_ge(rsq_done, t + 1)
                    before_tile(ve, qkt_ps, t)
                    dve.tensor_tensor(qkn[p][:].rearrange("p (h d) -> p h d", d=HD),
                                      b_qk[:, 0, :].rearrange("p (h d) -> p h d", d=HD),
                                      rsq[p][:, 1, :].unsqueeze(2).broadcast_to([P, 2 * HEADS, HD]),
                                      ALU.mult).then_inc(qkn_done, 1)
                if 2 in stages:
                    c = tile.back(2)
                    q = c.par
                    row = acc[:, bass.ds(c.t, 1), :].rearrange("p o d -> p (o d)")
                    ve.wait_ge(o_ps, c.t + 1)
                    dve.tensor_tensor(row, row, b_c[:, 0, D:2 * D], ALU.add).then_inc(x1_done, 1)
                    ve.wait_ge(x1_done, c.t + 1)
                    held(ve)
                    dve.bn_stats(st2[:], acc[:, bass.ds(c.t, 1), :]).then_inc(st2_done, 1)
                    ve.wait_ge(st2_done, c.t + 1)
                    before_tile(ve, rs2_done, c.t)
                    held(ve)
                    dve.bn_aggr(mv2[q][:], st2[:]).then_inc(mv2_done, 1)
                    ve.wait_ge(mv2_done, c.t + 1)
                    ve.wait_ge(rs2_done, c.t + 1)
                    before_tile(ve, x1nt_ps, c.t)
                    dve.tensor_scalar(x1n[q][:], row, mv2[q][:, 0:1], rs2[q][:, 1:2],
                                      ALU.subtract, ALU.mult).then_inc(x1n_done, 1)
                    ve.wait_ge(x1nt_done, c.t + 1)
                    cols = bass.ds(c.t * P, P)
                    dve.tensor_copy(xt_hi[:, :, cols], x1nt[q][:]).then_inc(hi_done, 1)
                    ve.wait_ge(hi_done, c.t + 1)
                    dve.tensor_tensor(xt_lo[:, :, cols], x1nt[q][:], xt_hi[:, :, cols].bitcast(f32),
                                      ALU.subtract).then_inc(lo_done, 1)

            run_tiles(ve, body)

            n = [0]

            def routed(ins):
                n[0] += 1
                ins.then_inc(route, 1)
                ve.wait_ge(route, n[0])

            def over_experts(v):
                return v[:].unsqueeze(2).broadcast_to([P, TILES, EXPERTS])

            ve.wait_ge(lg_done, TILES)
            ve.wait_ge(c_ps, TILES)
            ve.wait_ge(kbd_done, TILES)
            routed(dve.tensor_reduce(lmax[:], logits[:], AX.X, ALU.max))
            routed(dve.tensor_tensor(lex[:], logits[:], over_experts(lmax), ALU.subtract))
            ve.wait_ge(route_exp, 1)
            routed(dve.tensor_reduce(lsum[:], lex[:], AX.X, ALU.add))
            routed(dve.reciprocal(lrec[:], lsum[:]))
            routed(dve.tensor_tensor(prob[:], lex[:], over_experts(lrec), ALU.mult))
            full = [P, TILES, EXPERTS, EXPERTS]
            pj = prob[:].unsqueeze(2).broadcast_to(full)
            pe_ = prob[:].unsqueeze(3).broadcast_to(full)
            routed(dve.tensor_tensor(gt[:], pj, pe_, ALU.is_gt))
            routed(dve.tensor_tensor(eq[:], pj, pe_, ALU.is_equal))
            routed(dve.tensor_tensor(eq[:], eq[:], before_s[:].unsqueeze(1).broadcast_to(full), ALU.mult))
            routed(dve.tensor_tensor(gt[:], gt[:], eq[:], ALU.add))
            routed(dve.tensor_tensor(gt[:], gt[:], pj, ALU.mult))
            routed(dve.tensor_reduce(cum[:], gt[:], AX.X, ALU.add))
            routed(dve.tensor_scalar(cum[:], cum[:], TOP_P, 0.5, ALU.is_le, ALU.mult))
            routed(dve.tensor_tensor(weights[:], cum[:], prob[:], ALU.mult))
            routed(dve.tensor_copy(lmax[:], lsum[:]))
            assert n[0] == ROUTE_STEPS

            def inner(step, par):
                for m in range(MT):
                    k = step * MT + m
                    ve.wait_ge(tanh_done, k + 1)
                    dve.scalar_tensor_tensor(sg[m % 2][:], th[m % 2][:], 1.0, b_gate[m % 2][:, 0, :],
                                             ALU.add, ALU.mult).then_inc(sg_done, 1)
                    ve.wait_ge(up_ps, k + 1)
                    ve.wait_ge(sg_done, k + 1)
                    if not (isinstance(k, int) and k < 2):
                        ve.wait_ge(h_lo_done, k - 1)
                    dve.tensor_tensor(hf[m % 2][:], sg[m % 2][:], b_up[m % 2][:, 0, :], ALU.mult).then_inc(hf_done, 1)

            def accumulate(step, e, blk):
                for half in range(2):
                    ve.wait_ge(down_ps, step * 2 + half + 1)
                    for s in range(2):
                        tl = blk * TPB + (half * 2 + s)
                        row = acc[:, bass.ds(tl, 1), :].rearrange("p o d -> p (o d)")
                        l = dve.scalar_tensor_tensor(row, b_down[half][:, 0, s * D:(s + 1) * D],
                                                     weights[:, bass.ds(tl, 1), e:e + 1].rearrange("p o e -> p (o e)"),
                                                     row, ALU.mult, ALU.add)
                    if half == 1:
                        l.then_inc(acc_done, 1)
                    else:
                        l.then_inc(acc_half, 1)

            for e in range(EXPERTS):
                inner(e * BLOCKS, 0)
                if e:
                    accumulate(e * BLOCKS - 1, e - 1, BLOCKS - 1)
                inner(e * BLOCKS + 1, 1)
                accumulate(e * BLOCKS, e, 0)
                with ve.Fori(1, BLOCKS // 2) as j:
                    inner(2 * j + e * BLOCKS, 0)
                    accumulate(2 * j + (e * BLOCKS - 1), e, 2 * j - 1)
                    inner(2 * j + (e * BLOCKS + 1), 1)
                    accumulate(2 * j + e * BLOCKS, e, 2 * j)
            accumulate(EXPERTS * BLOCKS - 1, EXPERTS - 1, BLOCKS - 1)

        @block.tensor
        def _(pe):
            pe.wait_ge(prep, PREP_ALL)
            pe.wait_ge(const_in, 16 * 16)

            def body(tile, stages):
                t, p = tile.t, tile.par
                if 1 in stages:
                    a = tile.back(1)
                    ap = a.par
                    pe.wait_ge(kbd_done, a.t + 1)
                    pe.wait_ge(qkt_done, a.t + 1)
                    before_tile(pe, sub_done, a.t, ago=1)
                    for g in range(KD):
                        for b in range(BPT):
                            rows = slice(b * SEQ, (b + 1) * SEQ)
                            l = te.matmul(b_s[rows, g, :], qt[ap][:, g, rows],
                                          kbd[ap][:, b, g].rearrange("p h k -> p (h k)"), start=True, stop=True)
                    l.then_inc(s_ps, 1)
                    before_tile(pe, vbd_done, a.t, ago=1)
                    for b in range(BPT):
                        vals = b_v[:, 0, b * D:(b + 1) * D]
                        te.matmul(vals, cm[ap][:, 2 * b:2 * b + 2, :].rearrange("p b k -> p (b k)"), wkm_s[:, D:2 * D],
                                  start=True, stop=False)
                        l = te.matmul(vals, cd[ap][:, 2 * b:2 * b + 2, :].rearrange("p b k -> p (b k)"), wkd_s[:, D:2 * D],
                                      start=False, stop=True)
                    l.then_inc(v_ps, 1)
                if 0 in stages:
                    pe.wait_ge(ctx_in[p], (tile.i + 1) * 64)
                    before_tile(pe, qkn_done, t, ago=1)
                    keys = b_qk[:, 0, D:2 * D]
                    te.matmul(keys, cm[p][:, 1:1 + BPT, :].rearrange("p b k -> p (b k)"), wkm_s[:, 0:D], start=True, stop=False)
                    te.matmul(keys, cd[p][:, 1:1 + BPT, :].rearrange("p b k -> p (b k)"), wkd_s[:, 0:D], start=False, stop=False)
                    te.matmul(keys, rmask[:], bias_r[:, 1, :], start=False, stop=True)
                    pe.wait_ge(xn_done, t + 1)
                    before_tile(pe, xnt_done, t, ago=1)
                    before_tile(pe, x1nt_done, t, ago=3)
                    for k in range(KD):
                        l = te.transpose(b_x[:, 0, k * P:(k + 1) * P], xn[p][:, k * P:(k + 1) * P], ident_s[:])
                    l.then_inc(xnt_ps, 1)
                if 2 in stages:
                    c = tile.back(2)
                    q = c.par
                    pe.wait_ge(pn_done, c.t + 1)
                    for half in range(2):
                        before = 2 * c.t + half
                        if not (isinstance(before, int) and before < 1):
                            pe.wait_ge(pt_done, before)
                        for j in range(PAIRS // 2):
                            pair = half * (PAIRS // 2) + j
                            l = te.transpose(b_pt[:, 0, j * P:(j + 1) * P],
                                             pr[q][:, 2 * pair:2 * pair + 2, :].rearrange("p h k -> p (h k)"), ident_s[:])
                        l.then_inc(pt_ps, 1)
                if 0 in stages:
                    pe.wait_ge(xnt_done, t + 1)
                    for k in range(KD):
                        te.matmul(b_qk[:, 0, 0:D], xnt[p][:, k, :], wq_s[:, k, :], start=(k == 0), stop=False)
                    te.matmul(b_qk[:, 0, 0:D], rmask[:], bias_r[:, 0, :], start=False, stop=True).then_inc(qk_ps, 1)
                if 2 in stages:
                    pe.wait_ge(pt_done, 2 * c.t + 2)
                    pe.wait_ge(vbd_done, c.t + 1)
                    before_tile(pe, lg_done, c.t, ago=1)
                    for pair in range(PAIRS):
                        g, r = divmod(pair * 2 * HD, P)
                        for b in range(BPT):
                            l = te.matmul(b_c[r:r + 2 * HD, 0, g * P + b * SEQ:g * P + (b + 1) * SEQ],
                                          vbd[q][:, b, pair * 2 * HD:(pair + 1) * 2 * HD],
                                          pt[q][:, pair, b * SEQ:(b + 1) * SEQ], start=True, stop=True)
                    l.then_inc(c_ps, 1)
                if 0 in stages:
                    pe.wait_ge(qkn_done, t + 1)
                    before_tile(pe, qkt_done, t, ago=1)
                    for k in range(2 * KD):
                        l = te.transpose(b_qkt[:, 0, k * P:(k + 1) * P], qkn[p][:, k * P:(k + 1) * P], ident_s[:])
                    l.then_inc(qkt_ps, 1)
                if 2 in stages:
                    pe.wait_ge(ctxt_done, 2 * c.t + 2)
                    for g in range(KD):
                        te.matmul(b_c[:, 0, D:2 * D], ctxt[q][:, g, :], wo_s[:, g, :], start=(g == 0), stop=False)
                    te.matmul(b_c[:, 0, D:2 * D], rmask[:], bias_r[:, 2, :], start=False, stop=True).then_inc(o_ps, 1)
                    pe.wait_ge(x1n_done, c.t + 1)
                    for k in range(KD):
                        l = te.transpose(b_x[:, 0, D + k * P:D + (k + 1) * P], x1n[q][:, k * P:(k + 1) * P], ident_s[:])
                    l.then_inc(x1nt_ps, 1)
                    pe.wait_ge(x1nt_done, c.t + 1)
                    for k in range(KD):
                        l = te.matmul(b_c[:, 0, 0:EXPERTS], x1nt[q][:, k, :], rt_s[:, k, :], start=(k == 0), stop=(k == KD - 1))
                    l.then_inc(lg_ps, 1)

            run_tiles(pe, body)

            pe.wait_ge(lo_done, TILES)
            pe.wait_ge(lg_done, TILES)

            def gate_up(step, par, wp, blk):
                cols = bass.ds(blk * BLOCK, BLOCK)
                for m in range(MT):
                    n = step * MT + m
                    for which, b, s in ((0, b_gate[m % 2], gate_ps), (1, b_up[m % 2], up_ps)):
                        if not (isinstance(n, int) and n < 2):
                            pe.wait_ge(hf_done, n - 1)
                        first = True
                        for k in range(KD):
                            o = which * WPART + k * INNER + m * P
                            for w, xs in ((w_hi, xt_hi), (w_hi, xt_lo), (w_lo, xt_hi)):
                                l = te.matmul(b[:, 0, :], w[wp][:, o:o + P], xs[:, k, cols], start=first,
                                              stop=(k == KD - 1 and w is w_lo))
                                first = False
                        l.then_inc(s, 1)

            def down(step, par, wp):
                pe.wait_ge(h_lo_done, (step + 1) * MT)
                for half in range(2):
                    if not (isinstance(step, int) and step < 1):
                        pe.wait_ge(acc_half if half == 0 else acc_done, step)
                    for s in range(2):
                        tok = slice((half * 2 + s) * P, (half * 2 + s + 1) * P)
                        first = True
                        for k in range(MT):
                            o = 2 * WPART + k * D
                            for h, w in ((h_hi, w_hi), (h_hi, w_lo), (h_lo, w_hi)):
                                l = te.matmul(b_down[half][:, 0, s * D:(s + 1) * D], h[par][:, k, tok],
                                              w[wp][:, o:o + D], start=first, stop=(k == MT - 1 and h is h_lo))
                                first = False
                    l.then_inc(down_ps, 1)

            for e in range(EXPERTS):
                wp = e % 2
                pe.wait_ge(w_lo_done, 3 * (e + 1))
                gate_up(e * BLOCKS, 0, wp, 0)
                if e:
                    down(e * BLOCKS - 1, 1, 1 - wp)
                gate_up(e * BLOCKS + 1, 1, wp, 1)
                down(e * BLOCKS, 0, wp)
                with pe.Fori(1, BLOCKS // 2) as j:
                    gate_up(2 * j + e * BLOCKS, 0, wp, 2 * j)
                    down(2 * j + (e * BLOCKS - 1), 1, wp)
                    gate_up(2 * j + (e * BLOCKS + 1), 1, wp, 2 * j + 1)
                    down(2 * j + e * BLOCKS, 0, wp)
            down(EXPERTS * BLOCKS - 1, 1, (EXPERTS - 1) % 2)


def kernel(**inputs):
    import numpy as np
    import concourse.bacc as bacc
    from concourse import mybir as mb
    from concourse.bass_utils import run_bass_kernel_spmd

    a = {k.removeprefix("L0_").removeprefix("xattn_").removeprefix("ffn_"): np.asarray(v) for k, v in inputs.items()}

    def by_rows(w):
        return w.reshape(-1, P, w.shape[-1]).transpose(1, 0, 2)

    both = np.concatenate([a["Wk"], a["Wv"]], axis=1).reshape(CD, HEADS, 2, HD).transpose(0, 2, 1, 3)
    both_b = np.concatenate([a["bk"], a["bv"]]).reshape(HEADS, 2, HD).transpose(1, 0, 2).reshape(2, D)
    dca_b = a["bkv_dca"].reshape(2, D)
    main = (np.arange(P) % KEYS < KEYS_MAIN).astype(np.float32)
    experts = [w.transpose(0, 2, 1).reshape(EXPERTS, KD, P, INNER).transpose(0, 2, 1, 3).reshape(EXPERTS, P, -1)
               for w in (a["gate_w"], a["up_w"])]
    experts.append(a["down_w"].transpose(0, 2, 1).reshape(EXPERTS, MT, P, D).transpose(0, 2, 1, 3).reshape(EXPERTS, P, -1))
    e = np.arange(EXPERTS)
    arrays = {
        "x": a["x"].reshape(TOKENS, D),
        "ctx_t": a["ctx_1024"].reshape(BATCH * KEYS, CD).T,
        "wq": by_rows(a["Wq"]),
        "wkv_main": both.reshape(CD, 2 * D),
        "wkv_dca": a["Wkv_dca"],
        "wo": by_rows(a["Wo"]),
        "router": by_rows(a["router_w"].T),
        "w_ffn": np.concatenate(experts, axis=2),
        "ln_scales": np.stack([np.tile(a[n], HG) for n in ("qn_w", "qn_b", "kn_w", "kn_b", "kn_dca_w", "kn_dca_b")], axis=1),
        "q_bias": np.stack([a["bq"]] * 4),
        "k_bias": np.stack([both_b[0], dca_b[0]] * 2),
        "o_bias": np.stack([a["bo"]] * 4),
        "v_bias": np.stack([both_b[1].reshape(KD, P).T, dca_b[1].reshape(KD, P).T], axis=1),
        "ident": np.eye(P, dtype=np.float32),
        "head_mask": (np.arange(P)[:, None] // HD == np.arange(HG)).astype(np.float32),
        "pair_mask": (np.arange(P)[:, None] // KEYS == np.arange(D) // HD % 2).astype(np.float32),
        "row_mask": np.stack([main, 1 - main] * 2),
        "hi_lo_rows": np.array(HI_LO, np.float32),
        "before": np.broadcast_to((e[None, :] < e[:, None]).astype(np.float32), (P, EXPERTS, EXPERTS)),
    }
    nc = bacc.Bacc("TRN2", target_bir_lowering=False, num_devices=1)
    arrays = {n: np.ascontiguousarray(v) for n, v in arrays.items()}
    args = [nc.dram_tensor(n, v.shape, mb.dt.from_np(v.dtype), kind="ExternalInput").ap() for n, v in arrays.items()]
    args.append(nc.dram_tensor("out", (TOKENS, D), mb.dt.float32, kind="ExternalOutput").ap())
    xattn_ffn_kernel(nc, *args)
    r = run_bass_kernel_spmd(nc, [arrays], core_ids=[0])
    return r.results[0]["out"].reshape(BATCH, SEQ, D)
```

```python
import concourse.bass as bass
from concourse import mybir
from contextlib import ExitStack

BATCH, SEQ, D = 64, 64, 256
KEYS, KEYS_MAIN, CD = 64, 48, 128
HEADS, HD = 16, 16
EXPERTS, INNER = 8, 512
TOP_P = 0.9
P = 128
TOKENS = BATCH * SEQ
TILES = TOKENS // P
BPT = P // SEQ
KD = D // P
HG = P // HD
PAIRS = HEADS // 2
BLOCK = 512
BLOCKS = TOKENS // BLOCK
HI_LO = [[1, 0], [1, 0], [0, 1], [0, 1]]
TPB = BLOCK // P
MT = INNER // P
WPART = KD * INNER


def xattn_ffn_kernel(nc, x, ctx_t, wq, wkv_main, wkv_dca, wo, router, w_ffn, ln_scales,
                     q_bias, k_bias, o_bias, v_bias, ident, head_mask, pair_mask, row_mask,
                     hi_lo_rows, before, out):
    f32, f32r = mybir.dt.float32, mybir.dt.float32r
    ALU, ACT, AX = mybir.AluOpType, mybir.ActivationFunctionType, mybir.AxisListType
    dve, act_e, pool_e, te = nc.vector, nc.scalar, nc.gpsimd, nc.tensor

    whole = ExitStack()
    with whole:
        def sem(name):
            return whole.enter_context(nc.semaphore(name))

        def keep(name, shape, dt=f32):
            return whole.enter_context(nc.sbuf_tensor(name, shape, dt))

        acc = keep("acc", [P, TILES, D])
        xt_hi = keep("xt_hi", [P, KD, TOKENS], f32r)
        xt_lo = keep("xt_lo", [P, KD, TOKENS], f32r)
        logits = keep("logits", [P, TILES, EXPERTS])
        weights = keep("weights", [P, TILES, EXPERTS])
        before_s = keep("before_s", [P, EXPERTS, EXPERTS])

        phase = ExitStack()

        def sb(name, shape, dt=f32):
            return phase.enter_context(nc.sbuf_tensor(name, shape, dt))

        ident_s = sb("ident_s", [P, P])
        wq_s = sb("wq_s", [P, KD, D])
        wkm_s = sb("wkm_s", [P, 2 * D])
        wkd_s = sb("wkd_s", [P, 2 * D])
        wo_s = sb("wo_s", [P, KD, D])
        rt_s = sb("rt_s", [P, KD, EXPERTS])
        lnp = sb("lnp", [P, 6])
        vb_s = sb("vb_s", [P, 2, KD])
        vb_sum = sb("vb_sum", [P, KD])
        hmask = sb("hmask", [P, HG])
        pmask = sb("pmask", [P, D])
        rmask_f = sb("rmask_f", [4, P])
        rmask = sb("rmask", [4, P], f32r)
        hilo = sb("hilo", [4, 2])
        bias_f = sb("bias_f", [4, 3, D])
        bias_t = sb("bias_t", [4, 3, D])
        bias_h = sb("bias_h", [4, 3, D], f32r)
        bias_u = sb("bias_u", [4, 3, D])
        bias_r = sb("bias_r", [4, 3, D], f32r)
        gsum = sb("gsum", [P, 4, HEADS])
        gsum_b = sb("gsum_b", [4, 2, HEADS])
        minus_half = sb("minus_half", [P, 2 * HEADS])
        eps_model = sb("eps_model", [P, 1])
        eps_heads = sb("eps_heads", [P, 2 * HEADS])
        hold = sb("hold", [P, 3])

        cm = [sb(f"cm{p}", [P, BPT * 2, KEYS]) for p in (0, 1)]
        cd = [sb(f"cd{p}", [P, BPT * 2, KEYS]) for p in (0, 1)]
        st1, st2 = sb("st1", [P, 6]), sb("st2", [P, 6])
        mv1 = [sb(f"mv1{p}", [P, 2]) for p in (0, 1)]
        mv2 = [sb(f"mv2{p}", [P, 2]) for p in (0, 1)]
        rs1 = [sb(f"rs1{p}", [P, 2]) for p in (0, 1)]
        rs2 = [sb(f"rs2{p}", [P, 2]) for p in (0, 1)]
        xn = [sb(f"xn{p}", [P, D]) for p in (0, 1)]
        xnt = [sb(f"xnt{p}", [P, KD, P]) for p in (0, 1)]
        sq = [sb(f"sq{p}", [P, 2 * D]) for p in (0, 1)]
        ss = [sb(f"ss{p}", [P, 2 * HEADS]) for p in (0, 1)]
        rsq = [sb(f"rsq{p}", [P, 3, 2 * HEADS]) for p in (0, 1)]
        qkn = [sb(f"qkn{p}", [P, 2 * D]) for p in (0, 1)]
        vbd = [sb(f"vbd{p}", [P, BPT, D]) for p in (0, 1)]
        qt = [sb(f"qt{p}", [P, KD, P]) for p in (0, 1)]
        kt = [sb(f"kt{p}", [P, KD, BPT, KEYS]) for p in (0, 1)]
        kbd = [sb(f"kbd{p}", [P, BPT, KD, HG, KEYS]) for p in (0, 1)]
        mx = sb("mx", [P, 2, HEADS])
        sm = [sb(f"sm{p}", [P, 2, HEADS]) for p in (0, 1)]
        rc = [sb(f"rc{p}", [P, 2, HEADS]) for p in (0, 1)]
        pr = [sb(f"pr{p}", [P, HEADS, KEYS]) for p in (0, 1)]
        pt = [sb(f"pt{p}", [P, PAIRS, P]) for p in (0, 1)]
        ctxt = [sb(f"ctxt{p}", [P, KD, P]) for p in (0, 1)]
        x1n = [sb(f"x1n{p}", [P, D]) for p in (0, 1)]
        x1nt = [sb(f"x1nt{p}", [P, KD, P]) for p in (0, 1)]
        phase.close()

        phase = ExitStack()
        w_raw = sb("w_raw", [P, 3 * WPART])
        w_hi = [sb(f"w_hi{p}", [P, 3 * WPART], f32r) for p in (0, 1)]
        w_lo = [sb(f"w_lo{p}", [P, 3 * WPART], f32r) for p in (0, 1)]
        h_hi = [sb(f"h_hi{p}", [P, MT, BLOCK], f32r) for p in (0, 1)]
        h_lo = [sb(f"h_lo{p}", [P, MT, BLOCK], f32r) for p in (0, 1)]
        th = [sb(f"th{p}", [P, BLOCK]) for p in (0, 1)]
        sg = [sb(f"sg{p}", [P, BLOCK]) for p in (0, 1)]
        hf = [sb(f"hf{p}", [P, BLOCK]) for p in (0, 1)]
        phase.close()
        phase = ExitStack()
        lmax = sb("lmax", [P, TILES])
        lex = sb("lex", [P, TILES, EXPERTS])
        lsum = sb("lsum", [P, TILES])
        lrec = sb("lrec", [P, TILES])
        prob = sb("prob", [P, TILES, EXPERTS])
        gt = sb("gt", [P, TILES, EXPERTS, EXPERTS])
        eq = sb("eq", [P, TILES, EXPERTS, EXPERTS])
        cum = sb("cum", [P, TILES, EXPERTS])
        phase.close()

        def bank(stack, name, n=1):
            return stack.enter_context(nc.psum_tensor(name, [P, n, 512], f32))

        ps = ExitStack()
        b_qk = bank(ps, "b_qk")
        b_v = bank(ps, "b_v")
        b_x = bank(ps, "b_x")
        b_qkt = bank(ps, "b_qkt")
        b_s = bank(ps, "b_s", 2)
        b_pt = bank(ps, "b_pt")
        b_c = bank(ps, "b_c")
        ps.close()
        ps = ExitStack()
        b_gate = [bank(ps, f"b_gate{p}") for p in (0, 1)]
        b_up = [bank(ps, f"b_up{p}") for p in (0, 1)]
        b_down = [bank(ps, f"b_down{p}") for p in (0, 1)]
        ps.close()

        const_in, x_in = sem("const_in"), sem("x_in")
        zeroed = sem("zeroed")
        prep = sem("prep")
        ctx_in = [sem("ctx_in0"), sem("ctx_in1")]
        st1_done, mv1_done, rs1a_done, rs1_done = sem("st1_done"), sem("mv1_done"), sem("rs1a_done"), sem("rs1_done")
        xn_done, xnt_ps, xnt_done = sem("xn_done"), sem("xnt_ps"), sem("xnt_done")
        v_ps, qk_ps, sq_done, ss_done = sem("v_ps"), sem("qk_ps"), sem("sq_done"), sem("ss_done")
        ln_done, nr_done, rsqa_done, qkn_done, vbd_done = sem("ln_done"), sem("nr_done"), sem("rsqa_done"), sem("qkn_done"), sem("vbd_done")
        qkt_ps, qkt_done, kbd_done = sem("qkt_ps"), sem("qkt_done"), sem("kbd_done")
        s_ps, mx_done, sub_done, exp_done = sem("s_ps"), sem("mx_done"), sem("sub_done"), sem("exp_done")
        sm_done, rc_done, pn_done = sem("sm_done"), sem("rc_done"), sem("pn_done")
        pt_ps, pt_done, c_ps, ctxt_done = sem("pt_ps"), sem("pt_done"), sem("c_ps"), sem("ctxt_done")
        o_ps, x1_done, st2_done, mv2_done = sem("o_ps"), sem("x1_done"), sem("st2_done"), sem("mv2_done")
        rs2a_done, rs2_done, x1n_done = sem("rs2a_done"), sem("rs2_done"), sem("x1n_done")
        x1nt_ps, x1nt_done, lg_ps, lg_done = sem("x1nt_ps"), sem("x1nt_done"), sem("lg_ps"), sem("lg_done")
        hi_done, lo_done = sem("hi_done"), sem("lo_done")
        route, route_exp = sem("route"), sem("route_exp")
        w_in, w_hi_done, w_lo_done = sem("w_in"), sem("w_hi_done"), sem("w_lo_done")
        gate_ps, up_ps, tanh_done = sem("gate_ps"), sem("up_ps"), sem("tanh_done")
        sg_done, hf_done, h_hi_done, h_lo_done = sem("sg_done"), sem("hf_done"), sem("h_hi_done"), sem("h_lo_done")
        down_ps, acc_half, acc_done, stored = sem("down_ps"), sem("acc_half"), sem("acc_done"), sem("stored")

        ROUTE_STEPS = 14
        PREP_ALL = 16

        class Tile:
            def __init__(self, i, parity):
                self.i, self.par = i, parity
                self.t = 2 * i + parity

            def back(self, k):
                par = (self.par - k) % 2
                return Tile(self.i + (self.par - k - par) // 2, par)

        def before_tile(eng, s, t, per=1, ago=2, extra=0):
            if isinstance(t, int) and t - ago < 0:
                return
            eng.wait_ge(s, (t - ago + 1) * per + extra)

        STAGES = 6

        def run_tiles(eng, parts):
            def one(step):
                n = step.t if isinstance(step.t, int) else None
                for k, part in parts:
                    if n is None or 0 <= n - k < TILES:
                        part(step.back(k))

            first = (STAGES + 2) // 2 * 2
            for n in range(first):
                one(Tile(n // 2, n % 2))
            with eng.Fori(first // 2, TILES // 2) as i:
                for par in (0, 1):
                    one(Tile(i, par))
            for n in range(TILES, TILES + STAGES - 1):
                one(Tile(n // 2, n % 2))

        block = whole.enter_context(nc.Block())

        @block.sync
        def _(sp):
            for dst, src in ((ident_s[:], ident), (wq_s[:], wq), (wkm_s[:], wkv_main), (wkd_s[:], wkv_dca),
                             (wo_s[:], wo), (rt_s[:], router), (lnp[:], ln_scales), (vb_s[:], v_bias),
                             (hmask[:], head_mask), (pmask[:], pair_mask), (rmask_f[:], row_mask),
                             (hilo[:], hi_lo_rows), (before_s[:], before), (bias_f[:, 0, :], q_bias),
                             (bias_f[:, 1, :], k_bias), (bias_f[:, 2, :], o_bias)):
                sp.dma_start(dst, src).then_inc(const_in, 16)
            for t8 in range(4):
                n = TILES // 4
                sp.dma_start(acc[:, t8 * n:(t8 + 1) * n, :],
                             x[t8 * n * P:(t8 + 1) * n * P, :].rearrange("(t p) d -> p t d", p=P)).then_inc(x_in, 16)
            sp.wait_ge(zeroed, 1)

            def load_ctx(tile):
                before_tile(sp, v_ps, tile.t)
                b0 = tile.t * (BPT * KEYS)
                src = ctx_t[:, bass.ds(b0, BPT * KEYS)].rearrange("p (b k) -> p b k", k=KEYS)
                for buf, lo, hi in ((cm[tile.par], 0, KEYS_MAIN), (cd[tile.par], KEYS_MAIN, KEYS)):
                    for copy in range(2):
                        sp.dma_start(buf[:].rearrange("p (b c) k -> p b c k", c=2)[:, :, copy, lo:hi],
                                     src[:, :, lo:hi]).then_inc(ctx_in[tile.par], 16)

            load_ctx(Tile(0, 0))
            load_ctx(Tile(0, 1))
            with sp.Fori(1, TILES // 2) as i:
                load_ctx(Tile(i, 0))
                load_ctx(Tile(i, 1))

            sp.wait_ge(lo_done, TILES)
            sp.wait_ge(x1nt_ps, TILES)
            sp.wait_ge(lg_done, TILES)
            sp.wait_ge(route, ROUTE_STEPS)
            for e in range(EXPERTS):
                if e:
                    sp.wait_ge(w_lo_done, 3 * e)
                sp.dma_start(w_raw[:], w_ffn[e]).then_inc(w_in, 16)
            sp.wait_ge(acc_done, EXPERTS * BLOCKS)
            sp.dma_start(out.rearrange("(t p) d -> p t d", p=P), acc[:]).then_inc(stored, 16)
            sp.wait_ge(stored, 16)



        @block.gpsimd
        def _(pool):
            for n, b in enumerate(cm + cd):
                nc.gpsimd.memset(b[:], 0.0)
            nc.gpsimd.memset(eps_model[:], 1e-5)
            nc.gpsimd.memset(eps_heads[:], 1e-6 * HD)
            nc.gpsimd.memset(minus_half[:], -0.5).then_inc(zeroed, 1)
            pool.wait_ge(zeroed, 1)
            pool.wait_ge(const_in, 16 * 16)

            def normalise(tile):
                t, p = tile.t, tile.par
                pool.wait_ge(rc_done, t + 1)
                nc.gpsimd.tensor_tensor(pr[p][:, :, 0:KEYS_MAIN], pr[p][:, :, 0:KEYS_MAIN],
                                        rc[p][:, 0, :].unsqueeze(2).broadcast_to([P, HEADS, KEYS_MAIN]), ALU.mult)
                nc.gpsimd.tensor_tensor(pr[p][:, :, KEYS_MAIN:KEYS], pr[p][:, :, KEYS_MAIN:KEYS],
                                        rc[p][:, 1, :].unsqueeze(2).broadcast_to([P, HEADS, KEYS - KEYS_MAIN]),
                                        ALU.mult).then_inc(pn_done, 1)

            def rstd2(tile):
                t, p = tile.t, tile.par
                pool.wait_ge(mv2_done, t + 1)
                before_tile(pool, x1n_done, t)
                nc.gpsimd.tensor_tensor(rs2[p][:, 0:1], mv2[p][:, 1:2], eps_model[:], ALU.add).then_inc(rs2a_done, 1)
                pool.wait_ge(rs2a_done, t + 1)
                nc.gpsimd.tensor_tensor(rs2[p][:, 1:2], rs2[p][:, 0:1], minus_half[:, 0:1], ALU.pow).then_inc(rs2_done, 1)

            def rstd1(tile):
                t, p = tile.t, tile.par
                pool.wait_ge(mv1_done, t + 1)
                before_tile(pool, xn_done, t)
                nc.gpsimd.tensor_tensor(rs1[p][:, 0:1], mv1[p][:, 1:2], eps_model[:], ALU.add).then_inc(rs1a_done, 1)
                pool.wait_ge(rs1a_done, t + 1)
                nc.gpsimd.tensor_tensor(rs1[p][:, 1:2], rs1[p][:, 0:1], minus_half[:, 0:1], ALU.pow).then_inc(rs1_done, 1)

            def spread_keys(tile):
                t, p = tile.t, tile.par
                pool.wait_ge(qkt_done, t + 1)
                before_tile(pool, s_ps, t)
                for b in range(BPT):
                    l = nc.gpsimd.tensor_tensor(
                        kbd[p][:, b], kt[p][:, :, b, :].unsqueeze(2).broadcast_to([P, KD, HG, KEYS]),
                        hmask[:].unsqueeze(1).unsqueeze(3).broadcast_to([P, KD, HG, KEYS]), ALU.mult)
                l.then_inc(kbd_done, 1)

            run_tiles(pool,[(4, normalise), (5, rstd2), (0, rstd1), (2, spread_keys)])

            def split_weights(e):
                pool.wait_ge(w_in, 16 * (e + 1))
                for part in range(3):
                    pool.wait_ge(w_hi_done, 3 * e + part + 1)
                    if isinstance(e, int) and e >= 2 or not isinstance(e, int):
                        pool.wait_ge(down_ps, 2 * BLOCKS * (e - 1))
                    s = slice(part * WPART, (part + 1) * WPART)
                    nc.gpsimd.tensor_tensor(w_lo[e % 2][:, s], w_raw[:, s], w_hi[e % 2][:, s].bitcast(f32),
                                            ALU.subtract).then_inc(w_lo_done, 1)

            def rest(step, par):
                for m in range(MT):
                    n = step * MT + m
                    pool.wait_ge(h_hi_done, n + 1)
                    if not (isinstance(step, int) and step < 2):
                        pool.wait_ge(down_ps, 2 * (step - 1))
                    nc.gpsimd.tensor_tensor(h_lo[par][:, m, :], hf[m % 2][:], h_hi[par][:, m, :].bitcast(f32),
                                            ALU.subtract).then_inc(h_lo_done, 1)

            split_weights(0)
            for e in range(EXPERTS):
                rest(e * BLOCKS, 0)
                if e + 1 < EXPERTS:
                    pass
                rest(e * BLOCKS + 1, 1)
                if e + 1 < EXPERTS:
                    split_weights(e + 1)
                with pool.Fori(1, BLOCKS // 2) as j:
                    rest(2 * j + e * BLOCKS, 0)
                    rest(2 * j + (e * BLOCKS + 1), 1)

        @block.scalar
        def _(act):
            nc.scalar.preload_act_table_set("natural_log_exp_and_others")
            act.wait_ge(prep, PREP_ALL)

            def probs_t(tile, half):
                t, p = tile.t, tile.par
                hp = PAIRS // 2
                act.wait_ge(pt_ps, 2 * t + half + 1)
                before_tile(act, c_ps, t)
                nc.scalar.copy(pt[p][:, half * hp:(half + 1) * hp, :],
                               b_pt[:, 0, :].rearrange("p (j n) -> p j n", j=hp)).then_inc(pt_done, 1)

            def probs_t_first(tile):
                probs_t(tile, 0)

            def probs_t_second(tile):
                probs_t(tile, 1)

            def squares(tile):
                t, p = tile.t, tile.par
                act.wait_ge(qk_ps, t + 1)
                before_tile(act, ss_done, t)
                nc.scalar.activation(sq[p][:], b_qk[:, 0, :], ACT.Square).then_inc(sq_done, 1)

            def scale_shift(tile):
                t, p = tile.t, tile.par
                act.wait_ge(qkt_ps, t + 1)
                before_tile(act, s_ps, t)
                before_tile(act, kbd_done, t)
                w = b_qkt[:, 0, :].rearrange("p (a k b n) -> p a k b n", a=2, k=KD, b=BPT)
                nc.scalar.activation(qt[p][:], b_qkt[:, 0, 0:D].rearrange("p (k n) -> p k n", k=KD), ACT.Identity,
                                     bias=lnp[:, 1:2], scale=lnp[:, 0:1])
                nc.scalar.activation(kt[p][:, :, :, 0:KEYS_MAIN], w[:, 1, :, :, 0:KEYS_MAIN], ACT.Identity,
                                     bias=lnp[:, 3:4], scale=lnp[:, 2:3])
                nc.scalar.activation(kt[p][:, :, :, KEYS_MAIN:KEYS], w[:, 1, :, :, KEYS_MAIN:KEYS], ACT.Identity,
                                     bias=lnp[:, 5:6], scale=lnp[:, 4:5]).then_inc(qkt_done, 1)

            def exponentials(tile):
                t, p = tile.t, tile.par
                act.wait_ge(sub_done, t + 1)
                nc.scalar.activation(pr[p][:], pr[p][:], ACT.Exp, scale=HD ** -0.5).then_inc(exp_done, 1)

            def first_rstd(tile):
                t, p = tile.t, tile.par
                act.wait_ge(ss_done, t + 1)
                before_tile(act, qkn_done, t)
                nc.scalar.activation(rsq[p][:, 0, :], ss[p][:], ACT.Ln, bias=eps_heads[:, 0:1]).then_inc(ln_done, 1)
                act.wait_ge(ln_done, t + 1)
                nc.scalar.activation(rsq[p][:, 1, :], rsq[p][:, 0, :], ACT.Exp, scale=-0.5).then_inc(rsqa_done, 1)

            def evacuate_xnt(tile):
                t, p = tile.t, tile.par
                act.wait_ge(xnt_ps, t + 1)
                before_tile(act, qk_ps, t)
                nc.scalar.copy(xnt[p][:], b_x[:, 0, 0:D].rearrange("p (k n) -> p k n", k=KD)).then_inc(xnt_done, 1)

            def evacuate_x1nt(tile):
                t, p = tile.t, tile.par
                act.wait_ge(x1nt_ps, t + 1)
                before_tile(act, lg_ps, t)
                before_tile(act, lo_done, t)
                nc.scalar.copy(x1nt[p][:], b_x[:, 0, 0:D].rearrange("p (k n) -> p k n", k=KD)).then_inc(x1nt_done, 1)

            def evacuate_context(tile):
                t, p = tile.t, tile.par
                act.wait_ge(c_ps, t + 1)
                before_tile(act, o_ps, t)
                for g in range(KD):
                    nc.scalar.activation(ctxt[p][:, g, :], b_c[:, 0, g * P:(g + 1) * P], ACT.Identity,
                                         bias=vb_sum[:, g:g + 1]).then_inc(ctxt_done, 1)

            def evacuate_logits(tile):
                t, p = tile.t, tile.par
                act.wait_ge(lg_ps, t + 1)
                nc.scalar.copy(logits[:, bass.ds(t, 1), :], b_x[:, :, D:D + EXPERTS]).then_inc(lg_done, 1)

            run_tiles(act,[(1, squares), (2, scale_shift), (4, probs_t_first), (3, exponentials), (1, first_rstd),
                      (0, evacuate_xnt), (4, probs_t_second), (5, evacuate_x1nt), (4, evacuate_context), (5,
                      evacuate_logits)])

            act.wait_ge(route, 2)
            nc.scalar.activation(lex[:], lex[:], ACT.Exp).then_inc(route_exp, 1)

            def split_weights(e):
                act.wait_ge(w_in, 16 * (e + 1))
                if e >= 2:
                    act.wait_ge(down_ps, 2 * BLOCKS * (e - 1))
                if e:
                    act.wait_ge(w_lo_done, 3 * e)
                for part in range(3):
                    s = slice(part * WPART, (part + 1) * WPART)
                    nc.scalar.copy(w_hi[e % 2][:, s], w_raw[:, s]).then_inc(w_hi_done, 1)

            nc.scalar.preload_act_table_set("exp_and_others")

            def inner(step, par):
                for m in range(MT):
                    n = step * MT + m
                    act.wait_ge(gate_ps, n + 1)
                    if not (isinstance(n, int) and n < 2):
                        act.wait_ge(sg_done, n - 1)
                    nc.scalar.activation(th[m % 2][:], b_gate[m % 2][:, 0, :], ACT.Tanh, scale=0.5).then_inc(tanh_done, 1)
                    if m:
                        leading(n - 1, step, par, m - 1)
                leading(step * MT + MT - 1, step, par, MT - 1)

            def leading(n, step, par, m):
                act.wait_ge(hf_done, n + 1)
                if not (isinstance(step, int) and step < 2):
                    act.wait_ge(down_ps, 2 * (step - 1))
                nc.scalar.copy(h_hi[par][:, m, :], hf[m % 2][:]).then_inc(h_hi_done, 1)

            split_weights(0)
            for e in range(EXPERTS):
                inner(e * BLOCKS, 0)
                inner(e * BLOCKS + 1, 1)
                if e + 1 < EXPERTS:
                    split_weights(e + 1)
                with act.Fori(1, BLOCKS // 2) as j:
                    inner(2 * j + e * BLOCKS, 0)
                    inner(2 * j + (e * BLOCKS + 1), 1)

        @block.vector
        def _(ve):
            step = [0]

            def chained(ins):
                step[0] += 1
                ins.then_inc(prep, 1)
                ve.wait_ge(prep, step[0])

            ve.wait_ge(const_in, 16 * 16)
            chained(dve.tensor_reduce(gsum[:, 0:2, :], wq_s[:].rearrange("p k (h d) -> p k h d", d=HD), AX.X, ALU.add))
            chained(dve.tensor_reduce(gsum[:, 2, :], wkm_s[:, 0:D].rearrange("p (h d) -> p h d", d=HD), AX.X, ALU.add))
            chained(dve.tensor_reduce(gsum[:, 3, :], wkd_s[:, 0:D].rearrange("p (h d) -> p h d", d=HD), AX.X, ALU.add))
            chained(dve.tensor_scalar(gsum[:], gsum[:], 1.0 / HD, None, ALU.mult))

            def center(w, mean):
                v = w.rearrange("p (h d) -> p h d", d=HD)
                return dve.tensor_tensor(v, v, mean.unsqueeze(2).broadcast_to([v.shape[0], HEADS, HD]), ALU.subtract)

            for k in range(KD):
                center(wq_s[:, k, :], gsum[:, k, :])
            center(wkm_s[:, 0:D], gsum[:, 2, :])
            chained(center(wkd_s[:, 0:D], gsum[:, 3, :]))
            chained(dve.tensor_reduce(gsum_b[:], bias_f[:, 0:2, :].rearrange("p k (h d) -> p k h d", d=HD), AX.X, ALU.add))
            chained(dve.tensor_scalar(gsum_b[:], gsum_b[:], 1.0 / HD, None, ALU.mult))
            center(bias_f[:, 0, :], gsum_b[:, 0, :])
            chained(center(bias_f[:, 1, :], gsum_b[:, 1, :]))
            chained(dve.tensor_copy(bias_h[:], bias_f[:]))
            chained(dve.tensor_tensor(bias_t[:], bias_f[:], bias_h[:].bitcast(f32), ALU.subtract))
            chained(dve.tensor_scalar(bias_u[:], bias_h[:].bitcast(f32), hilo[:, 0:1], None, ALU.mult))
            chained(dve.tensor_scalar(bias_t[:], bias_t[:], hilo[:, 1:2], None, ALU.mult))
            chained(dve.tensor_tensor(bias_r[:], bias_u[:], bias_t[:], ALU.add))
            chained(dve.tensor_copy(rmask[:], rmask_f[:]))
            chained(dve.tensor_scalar(lnp[:, 0:6:2], lnp[:, 0:6:2], HD ** 0.5, None, ALU.mult))
            chained(dve.tensor_tensor(vb_sum[:], vb_s[:, 0, :], vb_s[:, 1, :], ALU.add))
            assert step[0] == PREP_ALL, step[0]
            ve.wait_ge(x_in, 4 * 16)

            def held(n):
                dve.memset(hold[:, n:n + 1], 0.0)

            sc = b_s[:].rearrange("p g (h k) -> p (g h) k", k=KEYS)
            parts = ((0, 0, KEYS_MAIN), (1, KEYS_MAIN, KEYS))

            def residual_stats(tile):
                t, p = tile.t, tile.par
                row = acc[:, bass.ds(t, 1), :].rearrange("p o d -> p (o d)")
                ve.wait_ge(o_ps, t + 1)
                dve.tensor_tensor(row, row, b_c[:, 0, D:2 * D], ALU.add).then_inc(x1_done, 1)
                ve.wait_ge(x1_done, t + 1)
                held(0)
                dve.bn_stats(st2[:], acc[:, bass.ds(t, 1), :]).then_inc(st2_done, 1)
                ve.wait_ge(st2_done, t + 1)
                before_tile(ve, rs2_done, t)
                held(1)
                dve.bn_aggr(mv2[p][:], st2[:]).then_inc(mv2_done, 1)

            def stats(tile):
                t, p = tile.t, tile.par
                dve.bn_stats(st1[:], acc[:, bass.ds(t, 1), :]).then_inc(st1_done, 1)
                ve.wait_ge(st1_done, t + 1)
                before_tile(ve, rs1_done, t)
                held(2)
                dve.bn_aggr(mv1[p][:], st1[:]).then_inc(mv1_done, 1)

            def subtract_max(tile):
                t, p = tile.t, tile.par
                ve.wait_ge(s_ps, t + 1)
                before_tile(ve, pt_ps, t, per=2)
                for n, lo, hi in parts:
                    l = dve.tensor_reduce(mx[:, n, :], sc[:, :, lo:hi], AX.X, ALU.max)
                l.then_inc(mx_done, 1)
                ve.wait_ge(mx_done, t + 1)
                for n, lo, hi in parts:
                    l = dve.tensor_tensor(pr[p][:, :, lo:hi], sc[:, :, lo:hi],
                                          mx[:, n, :].unsqueeze(2).broadcast_to([P, HEADS, hi - lo]), ALU.subtract)
                l.then_inc(sub_done, 1)

            def sum_squares(tile):
                t, p = tile.t, tile.par
                ve.wait_ge(sq_done, t + 1)
                before_tile(ve, ln_done, t)
                dve.tensor_reduce(ss[p][:], sq[p][:].rearrange("p (h d) -> p h d", d=HD), AX.X, ALU.add).then_inc(ss_done, 1)

            def normalise_x(tile):
                t, p = tile.t, tile.par
                ve.wait_ge(mv1_done, t + 1)
                ve.wait_ge(rs1_done, t + 1)
                before_tile(ve, xnt_ps, t)
                dve.tensor_scalar(xn[p][:], acc[:, bass.ds(t, 1), :].rearrange("p o d -> p (o d)"),
                                  mv1[p][:, 0:1], rs1[p][:, 1:2], ALU.subtract, ALU.mult).then_inc(xn_done, 1)

            def normalise_x1(tile):
                t, p = tile.t, tile.par
                ve.wait_ge(mv2_done, t + 1)
                ve.wait_ge(rs2_done, t + 1)
                before_tile(ve, x1nt_ps, t)
                dve.tensor_scalar(x1n[p][:], acc[:, bass.ds(t, 1), :].rearrange("p o d -> p (o d)"), mv2[p][:, 0:1], rs2[p][:, 1:2],
                                  ALU.subtract, ALU.mult).then_inc(x1n_done, 1)

            def values_diagonal(tile):
                t, p = tile.t, tile.par
                ve.wait_ge(v_ps, t + 1)
                before_tile(ve, c_ps, t)
                dve.tensor_tensor(vbd[p][:], b_v[:, 0, :].rearrange("p (b d) -> p b d", b=BPT),
                                  pmask[:].unsqueeze(1).broadcast_to([P, BPT, D]), ALU.mult).then_inc(vbd_done, 1)

            def normalise_heads(tile):
                t, p = tile.t, tile.par
                ve.wait_ge(rsqa_done, t + 1)
                v, y, w = rsq[p][:, 2, :], rsq[p][:, 1, :], rsq[p][:, 0, :]
                dve.tensor_tensor(v, ss[p][:], eps_heads[:], ALU.add)
                dve.scalar_tensor_tensor(w, y, -0.5, y, ALU.mult, ALU.mult).then_inc(nr_done, 1)
                ve.wait_ge(nr_done, 3 * t + 1)
                dve.tensor_tensor(v, v, w, ALU.mult).then_inc(nr_done, 1)
                ve.wait_ge(nr_done, 3 * t + 2)
                dve.scalar_tensor_tensor(w, v, 1.5, y, ALU.add, ALU.mult).then_inc(nr_done, 1)
                ve.wait_ge(nr_done, 3 * t + 3)
                before_tile(ve, qkt_ps, t)
                dve.tensor_tensor(qkn[p][:].rearrange("p (h d) -> p h d", d=HD),
                                  b_qk[:, 0, :].rearrange("p (h d) -> p h d", d=HD),
                                  w.unsqueeze(2).broadcast_to([P, 2 * HEADS, HD]), ALU.mult).then_inc(qkn_done, 1)

            def sums(tile):
                t, p = tile.t, tile.par
                ve.wait_ge(exp_done, t + 1)
                for n, lo, hi in parts:
                    l = dve.tensor_reduce(sm[p][:, n, :], pr[p][:, :, lo:hi], AX.X, ALU.add)
                l.then_inc(sm_done, 1)
                ve.wait_ge(sm_done, t + 1)
                before_tile(ve, pn_done, t)
                dve.reciprocal(rc[p][:], sm[p][:]).then_inc(rc_done, 1)

            def split_x1n(tile):
                t, p = tile.t, tile.par
                cols = bass.ds(t * P, P)
                ve.wait_ge(x1nt_done, t + 1)
                dve.tensor_copy(xt_hi[:, :, cols], x1nt[p][:]).then_inc(hi_done, 1)
                ve.wait_ge(hi_done, t + 1)
                dve.tensor_tensor(xt_lo[:, :, cols], x1nt[p][:], xt_hi[:, :, cols].bitcast(f32),
                                  ALU.subtract).then_inc(lo_done, 1)

            run_tiles(ve,[(5, residual_stats), (0, stats), (3, values_diagonal), (3, subtract_max), (0,
                      normalise_x), (1, sum_squares), (5, normalise_x1), (1, normalise_heads), (3, sums), (5,
                      split_x1n)])

            n = [0]

            def routed(ins):
                n[0] += 1
                ins.then_inc(route, 1)
                ve.wait_ge(route, n[0])

            def over_experts(v):
                return v[:].unsqueeze(2).broadcast_to([P, TILES, EXPERTS])

            ve.wait_ge(lg_done, TILES)
            ve.wait_ge(c_ps, TILES)
            ve.wait_ge(kbd_done, TILES)
            routed(dve.tensor_reduce(lmax[:], logits[:], AX.X, ALU.max))
            routed(dve.tensor_tensor(lex[:], logits[:], over_experts(lmax), ALU.subtract))
            ve.wait_ge(route_exp, 1)
            routed(dve.tensor_reduce(lsum[:], lex[:], AX.X, ALU.add))
            routed(dve.reciprocal(lrec[:], lsum[:]))
            routed(dve.tensor_tensor(prob[:], lex[:], over_experts(lrec), ALU.mult))
            full = [P, TILES, EXPERTS, EXPERTS]
            pj = prob[:].unsqueeze(2).broadcast_to(full)
            pe_ = prob[:].unsqueeze(3).broadcast_to(full)
            routed(dve.tensor_tensor(gt[:], pj, pe_, ALU.is_gt))
            routed(dve.tensor_tensor(eq[:], pj, pe_, ALU.is_equal))
            routed(dve.tensor_tensor(eq[:], eq[:], before_s[:].unsqueeze(1).broadcast_to(full), ALU.mult))
            routed(dve.tensor_tensor(gt[:], gt[:], eq[:], ALU.add))
            routed(dve.tensor_tensor(gt[:], gt[:], pj, ALU.mult))
            routed(dve.tensor_reduce(cum[:], gt[:], AX.X, ALU.add))
            routed(dve.tensor_scalar(cum[:], cum[:], TOP_P, 0.5, ALU.is_le, ALU.mult))
            routed(dve.tensor_tensor(weights[:], cum[:], prob[:], ALU.mult))
            routed(dve.tensor_copy(lmax[:], lsum[:]))
            assert n[0] == ROUTE_STEPS

            def inner(step, par):
                for m in range(MT):
                    k = step * MT + m
                    ve.wait_ge(tanh_done, k + 1)
                    dve.scalar_tensor_tensor(sg[m % 2][:], th[m % 2][:], 1.0, b_gate[m % 2][:, 0, :],
                                             ALU.add, ALU.mult).then_inc(sg_done, 1)
                    ve.wait_ge(up_ps, k + 1)
                    ve.wait_ge(sg_done, k + 1)
                    if not (isinstance(k, int) and k < 2):
                        ve.wait_ge(h_lo_done, k - 1)
                    dve.tensor_tensor(hf[m % 2][:], sg[m % 2][:], b_up[m % 2][:, 0, :], ALU.mult).then_inc(hf_done, 1)

            def accumulate(step, e, blk):
                for half in range(2):
                    ve.wait_ge(down_ps, step * 2 + half + 1)
                    for s in range(2):
                        tl = blk * TPB + (half * 2 + s)
                        row = acc[:, bass.ds(tl, 1), :].rearrange("p o d -> p (o d)")
                        l = dve.scalar_tensor_tensor(row, b_down[half][:, 0, s * D:(s + 1) * D],
                                                     weights[:, bass.ds(tl, 1), e:e + 1].rearrange("p o e -> p (o e)"),
                                                     row, ALU.mult, ALU.add)
                    if half == 1:
                        l.then_inc(acc_done, 1)
                    else:
                        l.then_inc(acc_half, 1)

            for e in range(EXPERTS):
                inner(e * BLOCKS, 0)
                if e:
                    accumulate(e * BLOCKS - 1, e - 1, BLOCKS - 1)
                inner(e * BLOCKS + 1, 1)
                accumulate(e * BLOCKS, e, 0)
                with ve.Fori(1, BLOCKS // 2) as j:
                    inner(2 * j + e * BLOCKS, 0)
                    accumulate(2 * j + (e * BLOCKS - 1), e, 2 * j - 1)
                    inner(2 * j + (e * BLOCKS + 1), 1)
                    accumulate(2 * j + e * BLOCKS, e, 2 * j)
            accumulate(EXPERTS * BLOCKS - 1, EXPERTS - 1, BLOCKS - 1)

        @block.tensor
        def _(pe):
            pe.wait_ge(prep, PREP_ALL)
            pe.wait_ge(const_in, 16 * 16)

            def probs_t(tile, half):
                t, p = tile.t, tile.par
                if half == 0:
                    pe.wait_ge(pn_done, t + 1)
                if not (isinstance(t, int) and t == 0 and half == 0):
                    pe.wait_ge(pt_done, 2 * t + half)
                for j in range(PAIRS // 2):
                    pair = half * (PAIRS // 2) + j
                    l = te.transpose(b_pt[:, 0, j * P:(j + 1) * P],
                                     pr[p][:, 2 * pair:2 * pair + 2, :].rearrange("p h k -> p (h k)"), ident_s[:])
                l.then_inc(pt_ps, 1)

            def probs_t_first(tile):
                probs_t(tile, 0)

            def probs_t_second(tile):
                probs_t(tile, 1)

            def project(tile):
                t, p = tile.t, tile.par
                pe.wait_ge(ctxt_done, 2 * t + 2)
                for g in range(KD):
                    te.matmul(b_c[:, 0, D:2 * D], ctxt[p][:, g, :], wo_s[:, g, :], start=(g == 0), stop=False)
                te.matmul(b_c[:, 0, D:2 * D], rmask[:], bias_r[:, 2, :], start=False, stop=True).then_inc(o_ps, 1)

            def scores(tile):
                t, p = tile.t, tile.par
                pe.wait_ge(kbd_done, t + 1)
                before_tile(pe, sub_done, t, ago=1)
                for g in range(KD):
                    for b in range(BPT):
                        rows = slice(b * SEQ, (b + 1) * SEQ)
                        l = te.matmul(b_s[rows, g, :], qt[p][:, g, rows],
                                      kbd[p][:, b, g].rearrange("p h k -> p (h k)"), start=True, stop=True)
                l.then_inc(s_ps, 1)

            def keys_queries(tile):
                t, p = tile.t, tile.par
                pe.wait_ge(ctx_in[p], (tile.i + 1) * 64)
                before_tile(pe, qkn_done, t, ago=1)
                keys = b_qk[:, 0, D:2 * D]
                te.matmul(keys, cm[p][:, 1:1 + BPT, :].rearrange("p b k -> p (b k)"), wkm_s[:, 0:D], start=True, stop=False)
                te.matmul(keys, cd[p][:, 1:1 + BPT, :].rearrange("p b k -> p (b k)"), wkd_s[:, 0:D], start=False, stop=False)
                te.matmul(keys, rmask[:], bias_r[:, 1, :], start=False, stop=True)
                pe.wait_ge(xnt_done, t + 1)
                for k in range(KD):
                    te.matmul(b_qk[:, 0, 0:D], xnt[p][:, k, :], wq_s[:, k, :], start=(k == 0), stop=False)
                te.matmul(b_qk[:, 0, 0:D], rmask[:], bias_r[:, 0, :], start=False, stop=True).then_inc(qk_ps, 1)

            def transpose_heads(tile):
                t, p = tile.t, tile.par
                pe.wait_ge(qkn_done, t + 1)
                before_tile(pe, qkt_done, t, ago=1)
                for k in range(2 * KD):
                    l = te.transpose(b_qkt[:, 0, k * P:(k + 1) * P], qkn[p][:, k * P:(k + 1) * P], ident_s[:])
                l.then_inc(qkt_ps, 1)

            def transpose_x(tile):
                t, p = tile.t, tile.par
                pe.wait_ge(xn_done, t + 1)
                before_tile(pe, xnt_done, t, ago=1)
                before_tile(pe, lg_done, t, ago=STAGES)
                for k in range(KD):
                    l = te.transpose(b_x[:, 0, k * P:(k + 1) * P], xn[p][:, k * P:(k + 1) * P], ident_s[:])
                l.then_inc(xnt_ps, 1)

            def values(tile):
                t, p = tile.t, tile.par
                before_tile(pe, vbd_done, t, ago=1)
                for b in range(BPT):
                    vals = b_v[:, 0, b * D:(b + 1) * D]
                    te.matmul(vals, cm[p][:, 2 * b:2 * b + 2, :].rearrange("p b k -> p (b k)"), wkm_s[:, D:2 * D],
                              start=True, stop=False)
                    l = te.matmul(vals, cd[p][:, 2 * b:2 * b + 2, :].rearrange("p b k -> p (b k)"), wkd_s[:, D:2 * D],
                                  start=False, stop=True)
                l.then_inc(v_ps, 1)

            def transpose_x1(tile):
                t, p = tile.t, tile.par
                pe.wait_ge(x1n_done, t + 1)
                before_tile(pe, lg_done, t, ago=1)
                if not isinstance(t, int) or t + STAGES <= TILES:
                    pe.wait_ge(xnt_done, t + STAGES)
                for k in range(KD):
                    l = te.transpose(b_x[:, 0, k * P:(k + 1) * P], x1n[p][:, k * P:(k + 1) * P], ident_s[:])
                l.then_inc(x1nt_ps, 1)

            def attend(tile):
                t, p = tile.t, tile.par
                pe.wait_ge(pt_done, 2 * t + 2)
                pe.wait_ge(vbd_done, t + 1)
                before_tile(pe, ctxt_done, t, per=2, ago=1)
                before_tile(pe, x1_done, t, ago=1)
                for pair in range(PAIRS):
                    g, row = divmod(pair * 2 * HD, P)
                    for b in range(BPT):
                        l = te.matmul(b_c[row:row + 2 * HD, 0, g * P + b * SEQ:g * P + (b + 1) * SEQ],
                                      vbd[p][:, b, pair * 2 * HD:(pair + 1) * 2 * HD],
                                      pt[p][:, pair, b * SEQ:(b + 1) * SEQ], start=True, stop=True)
                l.then_inc(c_ps, 1)

            def route_logits(tile):
                t, p = tile.t, tile.par
                pe.wait_ge(x1nt_done, t + 1)
                for k in range(KD):
                    l = te.matmul(b_x[:, 0, D:D + EXPERTS], x1nt[p][:, k, :], rt_s[:, k, :],
                                  start=(k == 0), stop=(k == KD - 1))
                l.then_inc(lg_ps, 1)

            run_tiles(pe,[(5, project), (3, scores), (1, keys_queries), (2, transpose_heads), (4, probs_t_first),
                      (4, probs_t_second), (0, transpose_x), (2, values), (5, transpose_x1), (4, attend), (5,
                      route_logits)])

            pe.wait_ge(lo_done, TILES)
            pe.wait_ge(lg_done, TILES)

            def gate_up(step, par, wp, blk):
                cols = bass.ds(blk * BLOCK, BLOCK)
                for m in range(MT):
                    n = step * MT + m
                    for which, b, s in ((0, b_gate[m % 2], gate_ps), (1, b_up[m % 2], up_ps)):
                        if not (isinstance(n, int) and n < 2):
                            pe.wait_ge(hf_done, n - 1)
                        first = True
                        for k in range(KD):
                            o = which * WPART + k * INNER + m * P
                            for w, xs in ((w_hi, xt_hi), (w_hi, xt_lo), (w_lo, xt_hi)):
                                l = te.matmul(b[:, 0, :], w[wp][:, o:o + P], xs[:, k, cols], start=first,
                                              stop=(k == KD - 1 and w is w_lo))
                                first = False
                        l.then_inc(s, 1)

            def down(step, par, wp):
                pe.wait_ge(h_lo_done, (step + 1) * MT)
                for half in range(2):
                    if not (isinstance(step, int) and step < 1):
                        pe.wait_ge(acc_half if half == 0 else acc_done, step)
                    for s in range(2):
                        tok = slice((half * 2 + s) * P, (half * 2 + s + 1) * P)
                        first = True
                        for k in range(MT):
                            o = 2 * WPART + k * D
                            for h, w in ((h_hi, w_hi), (h_hi, w_lo), (h_lo, w_hi)):
                                l = te.matmul(b_down[half][:, 0, s * D:(s + 1) * D], h[par][:, k, tok],
                                              w[wp][:, o:o + D], start=first, stop=(k == MT - 1 and h is h_lo))
                                first = False
                    l.then_inc(down_ps, 1)

            for e in range(EXPERTS):
                wp = e % 2
                pe.wait_ge(w_lo_done, 3 * (e + 1))
                gate_up(e * BLOCKS, 0, wp, 0)
                if e:
                    down(e * BLOCKS - 1, 1, 1 - wp)
                gate_up(e * BLOCKS + 1, 1, wp, 1)
                down(e * BLOCKS, 0, wp)
                with pe.Fori(1, BLOCKS // 2) as j:
                    gate_up(2 * j + e * BLOCKS, 0, wp, 2 * j)
                    down(2 * j + (e * BLOCKS - 1), 1, wp)
                    gate_up(2 * j + (e * BLOCKS + 1), 1, wp, 2 * j + 1)
                    down(2 * j + e * BLOCKS, 0, wp)
            down(EXPERTS * BLOCKS - 1, 1, (EXPERTS - 1) % 2)


def kernel(**inputs):
    import numpy as np
    import concourse.bacc as bacc
    from concourse import mybir as mb
    from concourse.bass_utils import run_bass_kernel_spmd

    a = {k.removeprefix("L0_").removeprefix("xattn_").removeprefix("ffn_"): np.asarray(v) for k, v in inputs.items()}

    def by_rows(w):
        return w.reshape(-1, P, w.shape[-1]).transpose(1, 0, 2)

    both = np.concatenate([a["Wk"], a["Wv"]], axis=1).reshape(CD, HEADS, 2, HD).transpose(0, 2, 1, 3)
    both_b = np.concatenate([a["bk"], a["bv"]]).reshape(HEADS, 2, HD).transpose(1, 0, 2).reshape(2, D)
    dca_b = a["bkv_dca"].reshape(2, D)
    main = (np.arange(P) % KEYS < KEYS_MAIN).astype(np.float32)
    experts = [w.transpose(0, 2, 1).reshape(EXPERTS, KD, P, INNER).transpose(0, 2, 1, 3).reshape(EXPERTS, P, -1)
               for w in (a["gate_w"], a["up_w"])]
    experts.append(a["down_w"].transpose(0, 2, 1).reshape(EXPERTS, MT, P, D).transpose(0, 2, 1, 3).reshape(EXPERTS, P, -1))
    e = np.arange(EXPERTS)
    arrays = {
        "x": a["x"].reshape(TOKENS, D),
        "ctx_t": a["ctx_1024"].reshape(BATCH * KEYS, CD).T,
        "wq": by_rows(a["Wq"]),
        "wkv_main": both.reshape(CD, 2 * D),
        "wkv_dca": a["Wkv_dca"],
        "wo": by_rows(a["Wo"]),
        "router": by_rows(a["router_w"].T),
        "w_ffn": np.concatenate(experts, axis=2),
        "ln_scales": np.stack([np.tile(a[n], HG) for n in ("qn_w", "qn_b", "kn_w", "kn_b", "kn_dca_w", "kn_dca_b")], axis=1),
        "q_bias": np.stack([a["bq"]] * 4),
        "k_bias": np.stack([both_b[0], dca_b[0]] * 2),
        "o_bias": np.stack([a["bo"]] * 4),
        "v_bias": np.stack([both_b[1].reshape(KD, P).T, dca_b[1].reshape(KD, P).T], axis=1),
        "ident": np.eye(P, dtype=np.float32),
        "head_mask": (np.arange(P)[:, None] // HD == np.arange(HG)).astype(np.float32),
        "pair_mask": (np.arange(P)[:, None] // KEYS == np.arange(D) // HD % 2).astype(np.float32),
        "row_mask": np.stack([main, 1 - main] * 2),
        "hi_lo_rows": np.array(HI_LO, np.float32),
        "before": np.broadcast_to((e[None, :] < e[:, None]).astype(np.float32), (P, EXPERTS, EXPERTS)),
    }
    nc = bacc.Bacc("TRN2", target_bir_lowering=False, num_devices=1)
    arrays = {n: np.ascontiguousarray(v) for n, v in arrays.items()}
    args = [nc.dram_tensor(n, v.shape, mb.dt.from_np(v.dtype), kind="ExternalInput").ap() for n, v in arrays.items()]
    args.append(nc.dram_tensor("out", (TOKENS, D), mb.dt.float32, kind="ExternalOutput").ap())
    xattn_ffn_kernel(nc, *args)
    r = run_bass_kernel_spmd(nc, [arrays], core_ids=[0])
    return r.results[0]["out"].reshape(BATCH, SEQ, D)
```

```python
import concourse.bass as bass
from concourse import mybir
from contextlib import ExitStack

BATCH, SEQ, D = 64, 64, 256
KEYS, KEYS_MAIN, CD = 64, 48, 128
HEADS, HD = 16, 16
EXPERTS, INNER = 8, 512
TOP_P = 0.9
P = 128
TOKENS = BATCH * SEQ
TILES = TOKENS // P
BPT = P // SEQ
KD = D // P
HG = P // HD
PAIRS = HEADS // 2
UNIT = 256
UT = UNIT // P
BLOCK = 2 * UNIT
BLOCKS = TOKENS // BLOCK
RUN = 4
BT = BLOCK // P
ROW = D + EXPERTS
LISTED = (EXPERTS * BLOCKS + BLOCKS + 2) * BT
LA, LB = 8, 16
MID = TOKENS // 2
HI_LO = [[1, 0], [1, 0], [0, 1], [0, 1]]
MT = INNER // P
WPART = KD * INNER


def xattn_ffn_kernel(nc, x, ctx_t, wq, wkv_main, wkv_dca, wo, router, w_ffn, ln_scales,
                     q_bias, k_bias, o_bias, v_bias, ident, head_mask, pair_mask, row_mask,
                     hi_lo_rows, before, lower, steps, out, rows):
    f32, f32r, f16, i32 = mybir.dt.float32, mybir.dt.float32r, mybir.dt.float16, mybir.dt.int32
    ALU, ACT, AX = mybir.AluOpType, mybir.ActivationFunctionType, mybir.AxisListType
    dve, act_e, pool_e, te = nc.vector, nc.scalar, nc.gpsimd, nc.tensor

    whole = ExitStack()
    with whole:
        def sem(name):
            return whole.enter_context(nc.semaphore(name))

        def keep(name, shape, dt=f32):
            return whole.enter_context(nc.sbuf_tensor(name, shape, dt))

        acc = keep("acc", [P, TILES, D])
        logits = keep("logits", [P, TILES, EXPERTS])
        weights = keep("weights", [P, TILES, EXPERTS])
        before_s = keep("before_s", [P, EXPERTS + 1, EXPERTS])
        lower_s = keep("lower_s", [P, 2, P])
        steps_s = keep("steps_s", [P, P + 3 * TILES + 2])
        ident_s = keep("ident_s", [P, P])
        zero_rows = keep("zero_rows", [P, ROW])
        listed = keep("listed", [P, LISTED], mybir.dt.int32)
        counts = keep("counts", [P, 2 * EXPERTS + 1], mybir.dt.int32)
        low_of, high_of = steps_s[:, 0:P], steps_s[:, P:P + TILES]
        token_of = steps_s[:, P + TILES:P + 2 * TILES]
        more_blocks = steps_s[:, P + 2 * TILES:P + 2 * TILES + BLOCKS - 1]
        pad_row, pad_shift = (steps_s[:, P + 3 * TILES + k:P + 3 * TILES + k + 1] for k in (0, 1))

        w_raw = keep("w_raw", [P, 3 * WPART])
        w_hi = [keep(f"w_hi{p}", [P, 3 * WPART], f32r) for p in (0, 1)]
        w_lo = [keep(f"w_lo{p}", [P, 3 * WPART], f32r) for p in (0, 1)]
        phase = ExitStack()

        def sb(name, shape, dt=f32):
            return phase.enter_context(nc.sbuf_tensor(name, shape, dt))

        wq_s = sb("wq_s", [P, KD, D])
        wkm_s = sb("wkm_s", [P, 2 * D])
        wkd_s = sb("wkd_s", [P, 2 * D])
        wo_s = sb("wo_s", [P, KD, D])
        rt_s = sb("rt_s", [P, KD, EXPERTS])
        lnp = sb("lnp", [P, 6])
        vb_s = sb("vb_s", [P, 2, KD])
        vb_sum = sb("vb_sum", [P, KD])
        hmask = sb("hmask", [P, HG])
        pmask = sb("pmask", [P, D])
        rmask_f = sb("rmask_f", [4, P])
        rmask = sb("rmask", [4, P], f32r)
        hilo = sb("hilo", [4, 2])
        bias_f = sb("bias_f", [4, 3, D])
        bias_t = sb("bias_t", [4, 3, D])
        bias_h = sb("bias_h", [4, 3, D], f32r)
        bias_u = sb("bias_u", [4, 3, D])
        bias_r = sb("bias_r", [4, 3, D], f32r)
        gsum = sb("gsum", [P, 4, HEADS])
        gsum_b = sb("gsum_b", [4, 2, HEADS])
        minus_half = sb("minus_half", [P, 2 * HEADS])
        eps_model = sb("eps_model", [P, 1])
        eps_heads = sb("eps_heads", [P, 2 * HEADS])
        hold = sb("hold", [P, 3])

        cm = [sb(f"cm{p}", [P, BPT * 2, KEYS]) for p in (0, 1)]
        cd = [sb(f"cd{p}", [P, BPT * 2, KEYS]) for p in (0, 1)]
        st1, st2 = sb("st1", [P, 6]), sb("st2", [P, 6])
        mv1 = [sb(f"mv1{p}", [P, 2]) for p in (0, 1)]
        mv2 = [sb(f"mv2{p}", [P, 2]) for p in (0, 1)]
        rs1 = [sb(f"rs1{p}", [P, 2]) for p in (0, 1)]
        rs2 = [sb(f"rs2{p}", [P, 2]) for p in (0, 1)]
        xn = [sb(f"xn{p}", [P, D]) for p in (0, 1)]
        xnt = [sb(f"xnt{p}", [P, KD, P]) for p in (0, 1)]
        sq = [sb(f"sq{p}", [P, 2 * D]) for p in (0, 1)]
        ss = [sb(f"ss{p}", [P, 2 * HEADS]) for p in (0, 1)]
        rsq = [sb(f"rsq{p}", [P, 3, 2 * HEADS]) for p in (0, 1)]
        qkn = [sb(f"qkn{p}", [P, 2 * D]) for p in (0, 1)]
        vbd = [sb(f"vbd{p}", [P, BPT, D]) for p in (0, 1)]
        qt = [sb(f"qt{p}", [P, KD, P]) for p in (0, 1)]
        kt = [sb(f"kt{p}", [P, KD, BPT, KEYS]) for p in (0, 1)]
        kbd = [sb(f"kbd{p}", [P, BPT, KD, HG, KEYS]) for p in (0, 1)]
        mx = sb("mx", [P, 2, HEADS])
        sm = [sb(f"sm{p}", [P, 2, HEADS]) for p in (0, 1)]
        rc = [sb(f"rc{p}", [P, 2, HEADS]) for p in (0, 1)]
        pr = [sb(f"pr{p}", [P, HEADS, KEYS]) for p in (0, 1)]
        pt = [sb(f"pt{p}", [P, PAIRS, P]) for p in (0, 1)]
        ctxt = [sb(f"ctxt{p}", [P, KD, P]) for p in (0, 1)]
        x1n = [sb(f"x1n{p}", [P, D]) for p in (0, 1)]
        x1nt = [sb(f"x1nt{p}", [P, KD, P]) for p in (0, 1)]
        phase.close()

        phase = ExitStack()
        gat = [sb(f"gat{p}", [P, UT, ROW]) for p in (0, 1)]
        xh = [sb(f"xh{p}", [P, KD, UNIT], f32r) for p in (0, 1)]
        xl = [sb(f"xl{p}", [P, KD, UNIT], f32r) for p in (0, 1)]
        wcol = [sb(f"wcol{p}", [P, UT, EXPERTS]) for p in (0, 1)]
        idx_g = [sb(f"idx_g{p}", [P, UT], mybir.dt.int32) for p in (0, 1)]
        idx_s = [sb(f"idx_s{p}", [P, UT], mybir.dt.int32) for p in (0, 1)]
        h_hi = [sb(f"h_hi{p}", [P, MT, UNIT], f32r) for p in (0, 1)]
        h_lo = [sb(f"h_lo{p}", [P, MT, UNIT], f32r) for p in (0, 1)]
        th = [sb(f"th{p}", [P, 2, UNIT]) for p in (0, 1)]
        sg = [sb(f"sg{p}", [P, 2, UNIT]) for p in (0, 1)]
        hf = [sb(f"hf{p}", [P, 2, UNIT]) for p in (0, 1)]
        y = [sb(f"y{p}", [P, UT, D]) for p in (0, 1)]
        list_f = sb("list_f", [P, 2, TILES])
        in_a = [sb(f"in_a{p}", [P, TILES, LA], f16) for p in (0, 1)]
        in_b = [sb(f"in_b{p}", [P, TILES, LB], f16) for p in (0, 1)]
        high_f = sb("high_f", [P, EXPERTS + 1, TILES])
        in_low = [sb(f"in_low{p}", [P, TILES, P], f16) for p in (0, 1)]
        in_high = [sb(f"in_high{p}", [P, TILES, 2, TILES], f16) for p in (0, 1)]
        lmax = sb("lmax", [P, TILES])
        lex = sb("lex", [P, TILES, EXPERTS])
        lsum = sb("lsum", [P, TILES])
        lrec = sb("lrec", [P, TILES])
        prob = sb("prob", [P, TILES, EXPERTS])
        gt = sb("gt", [P, TILES, EXPERTS, EXPERTS])
        cum = sb("cum", [P, TILES, EXPERTS])
        kept = sb("kept", [P, EXPERTS, TILES])
        upto = [sb(f"upto{p}", [P, EXPERTS, TILES]) for p in (0, 1)]
        rank = sb("rank", [P, EXPERTS, TILES])
        rank_i = sb("rank_i", [P, EXPERTS, TILES], i32)
        low_i = sb("low_i", [P, EXPERTS, TILES], i32)
        high_i = sb("high_i", [P, EXPERTS, TILES], i32)
        low_i2 = sb("low_i2", [P, EXPERTS, TILES], i32)
        low_f = [sb(f"low_f{k}", [P, EXPERTS + 1, TILES]) for k in (0, 1)]
        nb_cmp = sb("nb_cmp", [P, EXPERTS, BLOCKS - 1])
        nb_f = sb("nb_f", [P, EXPERTS])
        base_p = sb("base_p", [P, EXPERTS + 1, EXPERTS])
        base_f = sb("base_f", [P, EXPERTS + 1])
        phase.close()

        def bank(stack, name, n=1):
            return stack.enter_context(nc.psum_tensor(name, [P, n, 512], f32))

        ps = ExitStack()
        b_qk = bank(ps, "b_qk")
        b_v = bank(ps, "b_v")
        b_x = bank(ps, "b_x")
        b_qkt = bank(ps, "b_qkt")
        b_s = bank(ps, "b_s", 2)
        b_pt = bank(ps, "b_pt")
        b_c = bank(ps, "b_c")
        ps.close()
        ps = ExitStack()
        b_gate = [bank(ps, f"b_gate{p}") for p in (0, 1)]
        b_up = [bank(ps, f"b_up{p}") for p in (0, 1)]
        b_down = [bank(ps, f"b_down{p}") for p in (0, 1)]
        b_xt = bank(ps, "b_xt")
        b_rank = bank(ps, "b_rank")
        b_list = b_rank
        ps.close()

        w_attn_in, prep_in, const_in, x_in = sem("w_attn_in"), sem("prep_in"), sem("const_in"), sem("x_in")
        x_first = sem("x_first")
        zeroed = sem("zeroed")
        prep = sem("prep")
        ctx_in = [sem("ctx_in0"), sem("ctx_in1")]
        st1_done, mv1_done, rs1a_done, rs1_done = sem("st1_done"), sem("mv1_done"), sem("rs1a_done"), sem("rs1_done")
        xn_done, xnt_ps, xnt_done = sem("xn_done"), sem("xnt_ps"), sem("xnt_done")
        v_ps, qk_ps, sq_done, ss_done = sem("v_ps"), sem("qk_ps"), sem("sq_done"), sem("ss_done")
        ln_done, nr_done, rsqa_done = sem("ln_done"), sem("nr_done"), sem("rsqa_done")
        qkn_done, vbd_done = sem("qkn_done"), sem("vbd_done")
        qkt_ps, qkt_done, kbd_done = sem("qkt_ps"), sem("qkt_done"), sem("kbd_done")
        s_ps, mx_done, sub_done, exp_done = sem("s_ps"), sem("mx_done"), sem("sub_done"), sem("exp_done")
        sm_done, rc_done, pn_done = sem("sm_done"), sem("rc_done"), sem("pn_done")
        pt_ps, pt_done, c_ps, ctxt_done = sem("pt_ps"), sem("pt_done"), sem("c_ps"), sem("ctxt_done")
        o_ps, x1_done, st2_done, mv2_done = sem("o_ps"), sem("x1_done"), sem("st2_done"), sem("mv2_done")
        rs2a_done, rs2_done, x1n_done = sem("rs2a_done"), sem("rs2_done"), sem("x1n_done")
        x1nt_ps, x1nt_done, lg_ps, lg_done = sem("x1nt_ps"), sem("x1nt_done"), sem("lg_ps"), sem("lg_done")
        rows_out = [sem("rows_out0"), sem("rows_out1")]
        pool_goes_on = sem("pool_goes_on")
        x1_out, rest_out = sem("x1_out"), sem("rest_out")
        route, route_exp = sem("route"), sem("route_exp")
        w_in, w_hi_done, w_lo_done = sem("w_in"), sem("w_hi_done"), sem("w_lo_done")
        gate_ps, up_ps, tanh_done = sem("gate_ps"), sem("up_ps"), sem("tanh_done")
        sg_done, hf_done, h_hi_done, h_lo_done = sem("sg_done"), sem("hf_done"), sem("h_hi_done"), sem("h_lo_done")
        down_ps, y_done, added = sem("down_ps"), sem("y_done"), sem("added")
        rank_ps, low_v, low_g, high_v, list_ps, listing, listed_done, ab_done = (
            sem(n) for n in ("rank_ps", "low_v", "low_g", "high_v", "list_ps", "listing", "listed_done", "ab_done"))
        idx_g_done, gathered = sem("idx_g_done"), [sem("gathered0"), sem("gathered1")]
        xt_ps, xh_done, xl_done, wcol_done = (sem(n) for n in ("xt_ps", "xh_done", "xl_done", "wcol_done"))

        KEPT_STEP, WEIGHTS_STEP = 9, 11
        RANK_STEP = 34
        ROUTE_STEPS = 35
        LOW_V = TILES // 2
        PREP_ALL = 16

        class Tile:
            def __init__(self, i, parity):
                self.i, self.par = i, parity
                self.t = 2 * i + parity

            def back(self, k):
                par = (self.par - k) % 2
                return Tile(self.i + (self.par - k - par) // 2, par)

        def before_tile(eng, s, t, per=1, ago=2, extra=0):
            if isinstance(t, int) and t - ago < 0:
                return
            eng.wait_ge(s, (t - ago + 1) * per + extra)

        STAGES = 6
        FIRST = 4

        def run_tiles(eng, parts, behind_first=None):
            def one(step):
                n = step.t if isinstance(step.t, int) else None
                for k, part in parts:
                    if n is None or 0 <= n - k < TILES:
                        part(step.back(k))

            first = (STAGES + 2) // 2 * 2
            for n in range(first):
                one(Tile(n // 2, n % 2))
                if n == 0 and behind_first:
                    behind_first()
            with eng.Fori(first // 2, TILES // 2) as i:
                for par in (0, 1):
                    one(Tile(i, par))
            for n in range(TILES, TILES + STAGES - 1):
                one(Tile(n // 2, n % 2))

        def low_product(par, lo, hi):
            full = [P, hi - lo, LA, LB]
            a, b = in_a[par][:, lo:hi, :], in_b[par][:, lo:hi, :]
            return (in_low[par][:, lo:hi, :].rearrange("p t (a b) -> p t a b", b=LB),
                    a.unsqueeze(3).broadcast_to(full), b.unsqueeze(2).broadcast_to(full))

        class Unit(Tile):
            def ahead(self, k):
                par = (self.par + k) % 2
                return Unit(self.i + (self.par + k - par) // 2, par)

            def back(self, k):
                return self.ahead(-k)

            def first(self, n):
                return isinstance(self.t, int) and self.t < n

        def rest_weights(eng, e, wp, parts):
            for part in parts:
                eng.wait_ge(w_hi_done, 3 * e + part + 1)
                s = slice(part * WPART, (part + 1) * WPART)
                eng.tensor_tensor(w_lo[wp][:, s], w_raw[:, s], w_hi[wp][:, s].bitcast(f32),
                                  ALU.subtract).then_inc(w_lo_done, 1)

        def in_front(eng, e):
            if isinstance(e, int) and e == 0:
                return 0
            return eng.value_load(counts[0:1, bass.ds(EXPERTS + e, 1)], min_val=0, max_val=EXPERTS * BLOCKS - 1) + 1

        def run_experts(eng, unit, between=lambda *at: None):
            def expert(e, par_e, front):
                more = not (isinstance(e, int) and e == EXPERTS - 1)
                for par in (0, 1):
                    if par == 0 and more:
                        between(e, par_e, 0, front)
                    unit(Unit(front, par), e, e - 1 if par == 0 else e, par_e, 1 - par_e if par == 0 else par_e, more)
                    if more:
                        between(e, par_e, par + 1, front)
                here = eng.value_load(counts[0:1, bass.ds(e, 1)], min_val=1, max_val=BLOCKS)
                with eng.Fori(0, BLOCKS // RUN) as run:
                    with eng.If(run * RUN + 1 < here):
                        with eng.Fori(0, RUN) as k:
                            with eng.If(run * RUN + (k + 1) < here):
                                for par in (0, 1):
                                    unit(Unit(front + (run * RUN + (k + 1)), par), e, e, par_e, par_e, False)

            expert(0, 0, 0)
            with eng.Fori(0, EXPERTS // 2 - 1) as q:
                for k in (1, 2):
                    expert(2 * q + k, k % 2, in_front(eng, 2 * q + k))
            expert(EXPERTS - 1, 1, in_front(eng, EXPERTS - 1))
            return in_front(eng, EXPERTS)

        block = whole.enter_context(nc.Block())

        @block.sync
        def _(sp):
            for dst, src in ((wq_s[:], wq), (wkm_s[:], wkv_main), (wkd_s[:], wkv_dca)):
                sp.dma_start(dst, src).then_inc(w_attn_in, 16)
            for dst, src in ((bias_f[:, 0, :], q_bias), (bias_f[:, 1, :], k_bias), (bias_f[:, 2, :], o_bias),
                             (hilo[:], hi_lo_rows),
                             (rmask_f[:], row_mask), (lnp[:], ln_scales), (vb_s[:], v_bias)):
                sp.dma_start(dst, src).then_inc(prep_in, 16)
            for dst, src in ((ident_s[:], ident), (hmask[:], head_mask), (pmask[:], pair_mask)):
                sp.dma_start(dst, src).then_inc(const_in, 16)
            sp.wait_ge(zeroed, 1)

            def load_ctx(tile):
                before_tile(sp, v_ps, tile.t)
                b0 = tile.t * (BPT * KEYS)
                src = ctx_t[:, bass.ds(b0, BPT * KEYS)].rearrange("p (b k) -> p b k", k=KEYS)
                for buf, lo, hi in ((cm[tile.par], 0, KEYS_MAIN), (cd[tile.par], KEYS_MAIN, KEYS)):
                    for copy in range(2):
                        sp.dma_start(buf[:].rearrange("p (b c) k -> p b c k", c=2)[:, :, copy, lo:hi],
                                     src[:, :, lo:hi]).then_inc(ctx_in[tile.par], 16)

            def store_rows(tile):
                t, p = tile.t, tile.par
                sp.wait_ge(x1n_done, t + 1)
                sp.dma_start(rows[bass.ds(t * P, P), 0:D], x1n[p][:]).then_inc(rows_out[p], 16)
                sp.dma_start(out[bass.ds(t * P, P), :],
                             acc[:, bass.ds(t, 1), :].rearrange("p o d -> p (o d)")).then_inc(x1_out, 16)

            run_tiles(sp, [(0, load_ctx), (5, store_rows)])
            sp.dma_start(w_raw[:], w_ffn[0]).then_inc(w_in, 16)
            sp.dma_start(rows[TOKENS:TOKENS + P, :], zero_rows[:]).then_inc(rest_out, 16)
            sp.dma_start(out[TOKENS:TOKENS + P, :], zero_rows[:, 0:D]).then_inc(rest_out, 16)
            sp.wait_ge(route, WEIGHTS_STEP)
            sp.dma_start(rows[0:TOKENS, D:ROW].rearrange("(t p) e -> p t e", p=P), weights[:]).then_inc(rest_out, 16)

            with sp.Fori(1, EXPERTS) as e:
                sp.wait_ge(w_lo_done, 3 * e)
                sp.dma_start(w_raw[:], w_ffn[bass.ds(e, 1)].rearrange("o p n -> p (o n)")).then_inc(w_in, 16)

        @block.gpsimd
        def _(pool):
            for n, b in enumerate(cm + cd):
                nc.gpsimd.memset(b[:], 0.0)
            nc.gpsimd.memset(zero_rows[:], 0.0)
            nc.gpsimd.memset(eps_model[:], 1e-5)
            nc.gpsimd.memset(eps_heads[:], 1e-6 * HD)
            nc.gpsimd.memset(minus_half[:], -0.5).then_inc(zeroed, 1)
            pool.wait_ge(zeroed, 1)
            pool.wait_ge(const_in, 8 * 16)

            def normalise(tile):
                t, p = tile.t, tile.par
                pool.wait_ge(rc_done, t + 1)
                nc.gpsimd.tensor_tensor(pr[p][:, :, 0:KEYS_MAIN], pr[p][:, :, 0:KEYS_MAIN],
                                        rc[p][:, 0, :].unsqueeze(2).broadcast_to([P, HEADS, KEYS_MAIN]), ALU.mult)
                nc.gpsimd.tensor_tensor(pr[p][:, :, KEYS_MAIN:KEYS], pr[p][:, :, KEYS_MAIN:KEYS],
                                        rc[p][:, 1, :].unsqueeze(2).broadcast_to([P, HEADS, KEYS - KEYS_MAIN]),
                                        ALU.mult).then_inc(pn_done, 1)

            def rstd2(tile):
                t, p = tile.t, tile.par
                pool.wait_ge(mv2_done, t + 1)
                before_tile(pool, x1n_done, t)
                nc.gpsimd.tensor_tensor(rs2[p][:, 0:1], mv2[p][:, 1:2], eps_model[:], ALU.add).then_inc(rs2a_done, 1)
                pool.wait_ge(rs2a_done, t + 1)
                nc.gpsimd.tensor_tensor(rs2[p][:, 1:2], rs2[p][:, 0:1], minus_half[:, 0:1], ALU.pow).then_inc(rs2_done, 1)

            def rstd1(tile):
                t, p = tile.t, tile.par
                pool.wait_ge(mv1_done, t + 1)
                before_tile(pool, xn_done, t)
                nc.gpsimd.tensor_tensor(rs1[p][:, 0:1], mv1[p][:, 1:2], eps_model[:], ALU.add).then_inc(rs1a_done, 1)
                pool.wait_ge(rs1a_done, t + 1)
                nc.gpsimd.tensor_tensor(rs1[p][:, 1:2], rs1[p][:, 0:1], minus_half[:, 0:1], ALU.pow).then_inc(rs1_done, 1)

            def spread_keys(tile):
                t, p = tile.t, tile.par
                pool.wait_ge(qkt_done, t + 1)
                before_tile(pool, s_ps, t)
                for b in range(BPT):
                    l = nc.gpsimd.tensor_tensor(
                        kbd[p][:, b], kt[p][:, :, b, :].unsqueeze(2).broadcast_to([P, KD, HG, KEYS]),
                        hmask[:].unsqueeze(1).unsqueeze(3).broadcast_to([P, KD, HG, KEYS]), ALU.mult)
                l.then_inc(kbd_done, 1)

            run_tiles(pool, [(4, normalise), (5, rstd2), (0, rstd1), (2, spread_keys)])

            rest_weights(pool, 0, 0, range(3))

            pool.wait_ge(route, RANK_STEP)

            def held():
                pool.sem_inc(pool_goes_on, 1)

            def low_places(e, par, part):
                pool.wait_ge(ab_done, e + 1)
                if not isinstance(e, int) or e >= 2:
                    pool.wait_ge(list_ps, e - 1)
                held()
                nc.gpsimd.tensor_tensor(*low_product(par, part * LOW_V, (part + 1) * LOW_V), ALU.mult).then_inc(low_g, 1)

            low_places(0, 0, 0)

            pool.wait_ge(rest_out, 3 * 16)
            for p in (0, 1):
                pool.wait_ge(rows_out[p], 16 * TILES // 2)
            pool.wait_ge(x1_out, 16 * TILES)
            pool.wait_ge(route, ROUTE_STEPS)

            def gather(u):
                pool.wait_ge(idx_g_done, u.t + 1)
                if not u.first(2):
                    pool.wait_ge(xt_ps, u.t - 1)
                    pool.wait_ge(wcol_done, u.t - 1)
                held()
                for s in range(UT):
                    nc.gpsimd.indirect_dma_start(gat[u.par][:, s, :], None, rows,
                                                 bass.IndirectOffsetOnAxis(idx_g[u.par][:, s:s + 1], 0)
                                                 ).then_inc(gathered[u.par], 16)

            def add_rows(u, s):
                pool.wait_ge(y_done, u.t + 1)
                if not (s == 0 and u.first(1)):
                    pool.wait_ge(added, (UT * u.t + s) * 16)
                held()
                nc.gpsimd.indirect_dma_start(out, bass.IndirectOffsetOnAxis(idx_s[u.par][:, s:s + 1], 0),
                                             y[u.par][:, s, :], None, compute_op=ALU.add).then_inc(added, 16)

            def unit(u, e, e_before, wp, wp_before, spare):
                if spare:
                    low_places(e + 2, wp, u.par)
                gather(u.ahead(2))
                if not u.first(2):
                    add_rows(u.back(2), 1)
                if spare and u.par:
                    rest_weights(pool, e + 1, 1 - wp, (2,))
                if not u.first(1):
                    add_rows(u.back(1), 0)

            gather(Unit(0, 0))
            low_places(1, 1, 0)
            gather(Unit(0, 1))
            total = run_experts(pool, unit)
            add_rows(Unit(total, 0).back(2), 1)
            add_rows(Unit(total, 0).back(1), 0)
            add_rows(Unit(total, 0).back(1), 1)
            pool.wait_ge(added, 2 * UT * 16 * total)
            pool.wait_ge(gathered[0], UT * 16 * (total + 1))
            pool.wait_ge(gathered[1], UT * 16 * (total + 1))

        @block.scalar
        def _(act):
            def load_x(lo, hi, s):
                act.dma_start(acc[:, lo:hi, :], x[lo * P:hi * P, :].rearrange("(t p) d -> p t d", p=P)).then_inc(s, 16)

            load_x(0, FIRST, x_first)
            nc.scalar.preload_act_table_set("natural_log_exp_and_others")
            for dst, src in ((wo_s[:], wo), (rt_s[:], router), (before_s[:], before), (lower_s[:], lower),
                             (steps_s[:], steps)):
                act.dma_start(dst, src).then_inc(const_in, 16)
            act.wait_ge(prep_in, 7 * 16)
            act.wait_ge(ctx_in[0], 64)
            load_x(FIRST, TILES // 2, x_in)
            load_x(TILES // 2, TILES, x_in)

            def probs_t(tile, half):
                t, p = tile.t, tile.par
                hp = PAIRS // 2
                act.wait_ge(pt_ps, 2 * t + half + 1)
                before_tile(act, c_ps, t)
                nc.scalar.copy(pt[p][:, half * hp:(half + 1) * hp, :],
                               b_pt[:, 0, :].rearrange("p (j n) -> p j n", j=hp)).then_inc(pt_done, 1)

            def probs_t_first(tile):
                probs_t(tile, 0)

            def probs_t_second(tile):
                probs_t(tile, 1)

            def squares(tile):
                t, p = tile.t, tile.par
                act.wait_ge(qk_ps, t + 1)
                before_tile(act, ss_done, t)
                nc.scalar.activation(sq[p][:], b_qk[:, 0, :], ACT.Square).then_inc(sq_done, 1)

            def scale_shift(tile):
                t, p = tile.t, tile.par
                if isinstance(t, int) and t == 0:
                    act.wait_ge(prep, PREP_ALL)
                act.wait_ge(qkt_ps, t + 1)
                before_tile(act, s_ps, t)
                before_tile(act, kbd_done, t)
                w = b_qkt[:, 0, :].rearrange("p (a k b n) -> p a k b n", a=2, k=KD, b=BPT)
                nc.scalar.activation(qt[p][:], b_qkt[:, 0, 0:D].rearrange("p (k n) -> p k n", k=KD), ACT.Identity,
                                     bias=lnp[:, 1:2], scale=lnp[:, 0:1])
                nc.scalar.activation(kt[p][:, :, :, 0:KEYS_MAIN], w[:, 1, :, :, 0:KEYS_MAIN], ACT.Identity,
                                     bias=lnp[:, 3:4], scale=lnp[:, 2:3])
                nc.scalar.activation(kt[p][:, :, :, KEYS_MAIN:KEYS], w[:, 1, :, :, KEYS_MAIN:KEYS], ACT.Identity,
                                     bias=lnp[:, 5:6], scale=lnp[:, 4:5]).then_inc(qkt_done, 1)

            def exponentials(tile):
                t, p = tile.t, tile.par
                act.wait_ge(sub_done, t + 1)
                nc.scalar.activation(pr[p][:], pr[p][:], ACT.Exp, scale=HD ** -0.5).then_inc(exp_done, 1)

            def first_rstd(tile):
                t, p = tile.t, tile.par
                act.wait_ge(ss_done, t + 1)
                before_tile(act, qkn_done, t)
                nc.scalar.activation(rsq[p][:, 0, :], ss[p][:], ACT.Ln, bias=eps_heads[:, 0:1]).then_inc(ln_done, 1)
                act.wait_ge(ln_done, t + 1)
                nc.scalar.activation(rsq[p][:, 1, :], rsq[p][:, 0, :], ACT.Exp, scale=-0.5).then_inc(rsqa_done, 1)

            def evacuate_xnt(tile):
                t, p = tile.t, tile.par
                act.wait_ge(xnt_ps, t + 1)
                before_tile(act, qk_ps, t)
                nc.scalar.copy(xnt[p][:], b_x[:, 0, 0:D].rearrange("p (k n) -> p k n", k=KD)).then_inc(xnt_done, 1)

            def evacuate_x1nt(tile):
                t, p = tile.t, tile.par
                act.wait_ge(x1nt_ps, t + 1)
                before_tile(act, lg_ps, t)
                nc.scalar.copy(x1nt[p][:], b_x[:, 0, 0:D].rearrange("p (k n) -> p k n", k=KD)).then_inc(x1nt_done, 1)

            def evacuate_context(tile):
                t, p = tile.t, tile.par
                act.wait_ge(c_ps, t + 1)
                before_tile(act, o_ps, t)
                for g in range(KD):
                    nc.scalar.activation(ctxt[p][:, g, :], b_c[:, 0, g * P:(g + 1) * P], ACT.Identity,
                                         bias=vb_sum[:, g:g + 1]).then_inc(ctxt_done, 1)

            def evacuate_logits(tile):
                t, p = tile.t, tile.par
                act.wait_ge(lg_ps, t + 1)
                nc.scalar.copy(logits[:, bass.ds(t, 1), :], b_x[:, :, D:D + EXPERTS]).then_inc(lg_done, 1)

            run_tiles(act, [(1, squares), (2, scale_shift), (4, probs_t_first), (3, exponentials), (1, first_rstd),
                      (0, evacuate_xnt), (4, probs_t_second), (5, evacuate_x1nt), (4, evacuate_context), (5,
                      evacuate_logits)])

            def split_weights(e, wp, parts, free):
                act.wait_ge(w_in, 16 * (e + 1))
                if free is not None:
                    act.wait_ge(down_ps, free)
                for part in parts:
                    s = slice(part * WPART, (part + 1) * WPART)
                    nc.scalar.copy(w_hi[wp][:, s], w_raw[:, s]).then_inc(w_hi_done, 1)

            act.wait_ge(route, 2)
            nc.scalar.activation(lex[:], lex[:], ACT.Exp).then_inc(route_exp, 1)
            split_weights(0, 0, range(3), None)

            nc.scalar.preload_act_table_set("exp_and_others")

            def leading_rows(u):
                act.wait_ge(xt_ps, u.t + 1)
                if not u.first(2):
                    act.wait_ge(up_ps, 2 * (u.t - 1))
                nc.scalar.copy(xh[u.par][:], b_xt[:, 0, :].rearrange("p (k n) -> p k n", k=KD)).then_inc(xh_done, 1)

            def unit(u, e, e_before, wp, wp_before, spare):
                for half in range(2):
                    n = 2 * u.t + half
                    act.wait_ge(gate_ps, n + 1)
                    if not u.first(1):
                        act.wait_ge(sg_done, n - 1)
                    nc.scalar.activation(th[half][:], b_gate[half][:, 0, :].rearrange("p (m n) -> p m n", m=2),
                                         ACT.Tanh, scale=0.5).then_inc(tanh_done, 1)
                    act.wait_ge(hf_done, n + 1)
                    if not u.first(2):
                        act.wait_ge(down_ps, u.t - 1)
                    nc.scalar.copy(h_hi[u.par][:, 2 * half:2 * half + 2, :], hf[half][:]).then_inc(h_hi_done, 1)
                    if half == 0:
                        leading_rows(u.ahead(1))

            def between(e, par_e, when, front):
                if when:
                    split_weights(e + 1, 1 - par_e, (0, 1) if when == 1 else (2,),
                                  None if isinstance(e, int) and e == 0 else 2 * front)

            act.wait_ge(route, ROUTE_STEPS)
            leading_rows(Unit(0, 0))
            run_experts(act, unit, between)

        @block.vector
        def _(ve):
            step = [0]

            def chained(ins):
                step[0] += 1
                ins.then_inc(prep, 1)
                ve.wait_ge(prep, step[0])

            ve.wait_ge(w_attn_in, 3 * 16)
            chained(dve.tensor_reduce(gsum[:, 0:2, :], wq_s[:].rearrange("p k (h d) -> p k h d", d=HD), AX.X, ALU.add))
            chained(dve.tensor_reduce(gsum[:, 2, :], wkm_s[:, 0:D].rearrange("p (h d) -> p h d", d=HD), AX.X, ALU.add))
            chained(dve.tensor_reduce(gsum[:, 3, :], wkd_s[:, 0:D].rearrange("p (h d) -> p h d", d=HD), AX.X, ALU.add))
            chained(dve.tensor_scalar(gsum[:], gsum[:], 1.0 / HD, None, ALU.mult))

            def center(w, mean):
                v = w.rearrange("p (h d) -> p h d", d=HD)
                return dve.tensor_tensor(v, v, mean.unsqueeze(2).broadcast_to([v.shape[0], HEADS, HD]), ALU.subtract)

            for k in range(KD):
                center(wq_s[:, k, :], gsum[:, k, :])
            center(wkm_s[:, 0:D], gsum[:, 2, :])
            chained(center(wkd_s[:, 0:D], gsum[:, 3, :]))

            def biases():
                ve.wait_ge(prep_in, 7 * 16)
                ve.wait_ge(const_in, 8 * 16)
                chained(dve.tensor_reduce(gsum_b[:], bias_f[:, 0:2, :].rearrange("p k (h d) -> p k h d", d=HD),
                                          AX.X, ALU.add))
                chained(dve.tensor_scalar(gsum_b[:], gsum_b[:], 1.0 / HD, None, ALU.mult))
                center(bias_f[:, 0, :], gsum_b[:, 0, :])
                chained(center(bias_f[:, 1, :], gsum_b[:, 1, :]))
                chained(dve.tensor_copy(bias_h[:], bias_f[:]))
                chained(dve.tensor_tensor(bias_t[:], bias_f[:], bias_h[:].bitcast(f32), ALU.subtract))
                chained(dve.tensor_scalar(bias_u[:], bias_h[:].bitcast(f32), hilo[:, 0:1], None, ALU.mult))
                chained(dve.tensor_scalar(bias_t[:], bias_t[:], hilo[:, 1:2], None, ALU.mult))
                chained(dve.tensor_tensor(bias_r[:], bias_u[:], bias_t[:], ALU.add))
                chained(dve.tensor_copy(rmask[:], rmask_f[:]))
                chained(dve.tensor_scalar(lnp[:, 0:6:2], lnp[:, 0:6:2], HD ** 0.5, None, ALU.mult))
                chained(dve.tensor_tensor(vb_sum[:], vb_s[:, 0, :], vb_s[:, 1, :], ALU.add))
                assert step[0] == PREP_ALL, step[0]

            ve.wait_ge(x_first, 16)

            def held(n):
                dve.memset(hold[:, n:n + 1], 0.0)

            sc = b_s[:].rearrange("p g (h k) -> p (g h) k", k=KEYS)
            parts = ((0, 0, KEYS_MAIN), (1, KEYS_MAIN, KEYS))

            def residual_stats(tile):
                t, p = tile.t, tile.par
                row = acc[:, bass.ds(t, 1), :].rearrange("p o d -> p (o d)")
                ve.wait_ge(o_ps, t + 1)
                dve.tensor_tensor(row, row, b_c[:, 0, D:2 * D], ALU.add).then_inc(x1_done, 1)
                ve.wait_ge(x1_done, t + 1)
                held(0)
                dve.bn_stats(st2[:], acc[:, bass.ds(t, 1), :]).then_inc(st2_done, 1)
                ve.wait_ge(st2_done, t + 1)
                before_tile(ve, rs2_done, t)
                held(1)
                dve.bn_aggr(mv2[p][:], st2[:]).then_inc(mv2_done, 1)

            def stats(tile):
                t, p = tile.t, tile.par
                if isinstance(t, int) and t == FIRST:
                    ve.wait_ge(x_in, 2 * 16)
                dve.bn_stats(st1[:], acc[:, bass.ds(t, 1), :]).then_inc(st1_done, 1)
                ve.wait_ge(st1_done, t + 1)
                before_tile(ve, rs1_done, t)
                held(2)
                dve.bn_aggr(mv1[p][:], st1[:]).then_inc(mv1_done, 1)

            def subtract_max(tile):
                t, p = tile.t, tile.par
                ve.wait_ge(s_ps, t + 1)
                before_tile(ve, pt_ps, t, per=2)
                for n, lo, hi in parts:
                    l = dve.tensor_reduce(mx[:, n, :], sc[:, :, lo:hi], AX.X, ALU.max)
                l.then_inc(mx_done, 1)
                ve.wait_ge(mx_done, t + 1)
                for n, lo, hi in parts:
                    l = dve.tensor_tensor(pr[p][:, :, lo:hi], sc[:, :, lo:hi],
                                          mx[:, n, :].unsqueeze(2).broadcast_to([P, HEADS, hi - lo]), ALU.subtract)
                l.then_inc(sub_done, 1)

            def sum_squares(tile):
                t, p = tile.t, tile.par
                ve.wait_ge(sq_done, t + 1)
                before_tile(ve, ln_done, t)
                dve.tensor_reduce(ss[p][:], sq[p][:].rearrange("p (h d) -> p h d", d=HD), AX.X, ALU.add).then_inc(ss_done, 1)

            def normalise_x(tile):
                t, p = tile.t, tile.par
                ve.wait_ge(mv1_done, t + 1)
                ve.wait_ge(rs1_done, t + 1)
                before_tile(ve, xnt_ps, t)
                dve.tensor_scalar(xn[p][:], acc[:, bass.ds(t, 1), :].rearrange("p o d -> p (o d)"),
                                  mv1[p][:, 0:1], rs1[p][:, 1:2], ALU.subtract, ALU.mult).then_inc(xn_done, 1)

            def normalise_x1(tile):
                t, p = tile.t, tile.par
                ve.wait_ge(mv2_done, t + 1)
                ve.wait_ge(rs2_done, t + 1)
                before_tile(ve, x1nt_ps, t)
                if not isinstance(t, int) or t >= 2:
                    ve.wait_ge(rows_out[p], tile.i * 16)
                dve.tensor_scalar(x1n[p][:], acc[:, bass.ds(t, 1), :].rearrange("p o d -> p (o d)"),
                                  mv2[p][:, 0:1], rs2[p][:, 1:2], ALU.subtract, ALU.mult).then_inc(x1n_done, 1)

            def values_diagonal(tile):
                t, p = tile.t, tile.par
                ve.wait_ge(v_ps, t + 1)
                before_tile(ve, c_ps, t)
                dve.tensor_tensor(vbd[p][:], b_v[:, 0, :].rearrange("p (b d) -> p b d", b=BPT),
                                  pmask[:].unsqueeze(1).broadcast_to([P, BPT, D]), ALU.mult).then_inc(vbd_done, 1)

            def normalise_heads(tile):
                t, p = tile.t, tile.par
                ve.wait_ge(rsqa_done, t + 1)
                v, y, w = rsq[p][:, 2, :], rsq[p][:, 1, :], rsq[p][:, 0, :]
                dve.tensor_tensor(v, ss[p][:], eps_heads[:], ALU.add)
                dve.scalar_tensor_tensor(w, y, -0.5, y, ALU.mult, ALU.mult).then_inc(nr_done, 1)
                ve.wait_ge(nr_done, 3 * t + 1)
                dve.tensor_tensor(v, v, w, ALU.mult).then_inc(nr_done, 1)
                ve.wait_ge(nr_done, 3 * t + 2)
                dve.scalar_tensor_tensor(w, v, 1.5, y, ALU.add, ALU.mult).then_inc(nr_done, 1)
                ve.wait_ge(nr_done, 3 * t + 3)
                before_tile(ve, qkt_ps, t)
                dve.tensor_tensor(qkn[p][:].rearrange("p (h d) -> p h d", d=HD),
                                  b_qk[:, 0, :].rearrange("p (h d) -> p h d", d=HD),
                                  w.unsqueeze(2).broadcast_to([P, 2 * HEADS, HD]), ALU.mult).then_inc(qkn_done, 1)

            def sums(tile):
                t, p = tile.t, tile.par
                ve.wait_ge(exp_done, t + 1)
                for n, lo, hi in parts:
                    l = dve.tensor_reduce(sm[p][:, n, :], pr[p][:, :, lo:hi], AX.X, ALU.add)
                l.then_inc(sm_done, 1)
                ve.wait_ge(sm_done, t + 1)
                before_tile(ve, pn_done, t)
                dve.reciprocal(rc[p][:], sm[p][:]).then_inc(rc_done, 1)

            run_tiles(ve, [(5, residual_stats), (0, stats), (3, subtract_max), (0, normalise_x), (3,
                      values_diagonal), (1, sum_squares), (5, normalise_x1), (1, normalise_heads), (3, sums)], biases)

            n = [0]

            def routed(ins):
                n[0] += 1
                ins.then_inc(route, 1)
                ve.wait_ge(route, n[0])

            def over_experts(v):
                return v[:].unsqueeze(2).broadcast_to([P, TILES, EXPERTS])

            ve.wait_ge(lg_done, TILES)
            ve.wait_ge(c_ps, TILES)
            ve.wait_ge(kbd_done, TILES)
            routed(dve.tensor_reduce(lmax[:], logits[:], AX.X, ALU.max))
            routed(dve.tensor_tensor(lex[:], logits[:], over_experts(lmax), ALU.subtract))
            ve.wait_ge(route_exp, 1)
            routed(dve.tensor_reduce(lsum[:], lex[:], AX.X, ALU.add))
            routed(dve.reciprocal(lrec[:], lsum[:]))
            routed(dve.tensor_tensor(prob[:], lex[:], over_experts(lrec), ALU.mult))
            for p in (0, 1):
                ve.wait_ge(rows_out[p], 16 * TILES // 2)
            for e in range(EXPERTS):
                for lo, hi, over in ((0, e, ALU.is_ge), (e, EXPERTS, ALU.is_gt)):
                    if hi > lo:
                        l = dve.tensor_tensor(gt[:, :, e, lo:hi], prob[:, :, lo:hi],
                                              prob[:, :, e:e + 1].broadcast_to([P, TILES, hi - lo]), over)
            routed(l)
            routed(dve.tensor_tensor(gt[:], gt[:], prob[:].unsqueeze(2).broadcast_to([P, TILES, EXPERTS, EXPERTS]),
                                     ALU.mult))
            routed(dve.tensor_reduce(cum[:], gt[:], AX.X, ALU.add))
            routed(dve.tensor_scalar(kept[:].rearrange("p e t -> p t e"), cum[:], TOP_P, None, ALU.is_le))
            assert n[0] == KEPT_STEP
            routed(dve.tensor_scalar(cum[:], cum[:], TOP_P, 0.5, ALU.is_le, ALU.mult))
            routed(dve.tensor_tensor(weights[:], cum[:], prob[:], ALU.mult))
            assert n[0] == WEIGHTS_STEP

            ve.wait_ge(rank_ps, 1)
            in_tile = b_rank[:, 0, 0:EXPERTS * TILES].rearrange("p (e t) -> p e t", t=TILES)
            of_tile = b_rank[:, 0, EXPERTS * TILES:].rearrange("p (e t) -> p e t", t=TILES)
            routed(dve.tensor_copy(upto[0][:], of_tile))
            k = 0
            while 2 ** k < TILES:
                a, b, w = upto[k % 2], upto[1 - k % 2], 2 ** k
                dve.tensor_copy(b[:, :, 0:w], a[:, :, 0:w])
                routed(dve.tensor_tensor(b[:, :, w:], a[:, :, w:], a[:, :, 0:TILES - w], ALU.add))
                k += 1
            upto_all = upto[k % 2]
            routed(dve.tensor_tensor(rank[:], upto_all[:], of_tile, ALU.subtract))
            routed(dve.tensor_tensor(rank[:], rank[:], in_tile, ALU.add))
            shape = [P, EXPERTS, BLOCKS - 1]
            routed(dve.tensor_tensor(nb_cmp[:], upto_all[:, :, TILES - 1:TILES].broadcast_to(shape),
                                     more_blocks.unsqueeze(1).broadcast_to(shape), ALU.is_gt))
            routed(dve.tensor_reduce(nb_f[:], nb_cmp[:], AX.X, ALU.add))
            routed(dve.tensor_scalar(nb_f[:], nb_f[:], 1.0, None, ALU.add))
            routed(dve.tensor_tensor(base_p[:], before_s[:], nb_f[:].unsqueeze(1).broadcast_to([P, EXPERTS + 1, EXPERTS]),
                                     ALU.mult))
            routed(dve.tensor_reduce(base_f[:], base_p[:], AX.X, ALU.add))
            routed(dve.tensor_copy(counts[:, 0:EXPERTS], nb_f[:]))
            routed(dve.tensor_scalar(counts[:, EXPERTS:], base_f[:], -1.0, None, ALU.add))
            routed(dve.tensor_copy(rank_i[:], rank[:]))
            routed(dve.tensor_scalar(low_i[:], rank_i[:], LB.bit_length() - 1, LA - 1, ALU.logical_shift_right,
                                     ALU.bitwise_and))
            routed(dve.tensor_scalar(low_i2[:], rank_i[:], LB - 1, None, ALU.bitwise_and))
            routed(dve.tensor_scalar(high_i[:], rank_i[:], P.bit_length() - 1, None, ALU.logical_shift_right))
            routed(dve.tensor_copy(low_f[0][:, 0:EXPERTS, :], low_i[:]))
            routed(dve.tensor_copy(low_f[1][:, 0:EXPERTS, :], low_i2[:]))
            for v in (high_f, low_f[0], low_f[1]):
                dve.memset(v[:, EXPERTS:EXPERTS + 1], 0.0)
            routed(dve.tensor_copy(high_f[:, 0:EXPERTS, :], high_i[:]))
            routed(dve.scalar_tensor_tensor(high_f[:, 0:EXPERTS, :], high_f[:, 0:EXPERTS, :], 1.0, kept[:],
                                            ALU.add, ALU.mult))
            assert n[0] == RANK_STEP, n[0]

            def of(v, e):
                return v[:, bass.ds(e, 1), :].rearrange("p o t -> p (o t)").unsqueeze(2)

            def low_factors(e, par):
                if not isinstance(e, int) or e >= 2:
                    ve.wait_ge(list_ps, e - 1)
                for v, oh, k in ((low_f[0], in_a, LA), (low_f[1], in_b, LB)):
                    l = dve.tensor_tensor(oh[par][:], of(v, e).broadcast_to([P, TILES, k]),
                                          low_of[:, 0:k].unsqueeze(1).broadcast_to([P, TILES, k]), ALU.is_equal)
                l.then_inc(ab_done, 1)

            def tile_places(e, par):
                full = [P, TILES, TILES]
                dve.tensor_tensor(in_high[par][:, :, 1, :], of(high_f, e).broadcast_to(full),
                                  high_of.unsqueeze(1).broadcast_to(full), ALU.is_equal).then_inc(high_v, 1)

            def numbers_there(e, par):
                ve.wait_ge(high_v, 2 * e + 1)
                dve.tensor_tensor(in_high[par][:, :, 0, :], in_high[par][:, :, 1, :],
                                  token_of.unsqueeze(2).broadcast_to([P, TILES, TILES]), ALU.mult).then_inc(high_v, 1)

            def fill_list(e, par, front):
                ve.wait_ge(list_ps, e + 1)
                number = b_list[:, 0, par * 2 * TILES:(par + 1) * 2 * TILES]
                dve.tensor_scalar(list_f[:, par, :], number[:, TILES:2 * TILES], pad_shift, pad_row, ALU.mult,
                                  ALU.add).then_inc(listing, 1)
                ve.wait_ge(listing, e + 1)
                if not isinstance(e, int) or e:
                    ve.wait_ge(listed_done, e)
                dve.tensor_tensor(listed[:, bass.ds(BT * front, TILES)], list_f[:, par, :], number[:, 0:TILES],
                                  ALU.add).then_inc(listed_done, 1)
                ve.wait_ge(listed_done, e + 1)

            routed(dve.tensor_copy(listed[:], pad_row.broadcast_to([P, LISTED])))
            assert n[0] == ROUTE_STEPS, n[0]

            def indices(u):
                if not u.first(2):
                    ve.wait_ge(gathered[u.par], UT * 16 * u.i)
                dve.tensor_copy(idx_g[u.par][:], listed[:, bass.ds(UT * u.t, UT)]).then_inc(idx_g_done, 1)

            def rest_rows(u):
                ve.wait_ge(xh_done, u.t + 1)
                if not u.first(2):
                    ve.wait_ge(up_ps, 2 * (u.t - 1))
                dve.tensor_tensor(xl[u.par][:], b_xt[:, 0, :].rearrange("p (k n) -> p k n", k=KD),
                                  xh[u.par][:].bitcast(f32), ALU.subtract).then_inc(xl_done, 1)

            def row_weights(u):
                ve.wait_ge(gathered[u.par], UT * 16 * (u.i + 1))
                if not u.first(2):
                    ve.wait_ge(y_done, u.t - 1)
                dve.tensor_copy(wcol[u.par][:], gat[u.par][:, :, D:ROW]).then_inc(wcol_done, 1)

            def weigh(u, e):
                ve.wait_ge(down_ps, u.t + 1)
                ve.wait_ge(wcol_done, u.t + 1)
                if not u.first(2):
                    ve.wait_ge(added, (UT * (u.t - 1)) * 16)
                dve.tensor_copy(idx_s[u.par][:], listed[:, bass.ds(UT * u.t, UT)])
                for s in range(UT):
                    l = dve.tensor_scalar(y[u.par][:, s, :], b_down[u.par][:, 0, s * D:(s + 1) * D],
                                          wcol[u.par][:, s, bass.ds(e, 1)], None, ALU.mult)
                l.then_inc(y_done, 1)

            def rest_inner(u, half):
                ve.wait_ge(h_hi_done, 2 * u.t + half + 1)
                if not u.first(2):
                    ve.wait_ge(down_ps, u.t - 1)
                dve.tensor_tensor(h_lo[u.par][:, 2 * half:2 * half + 2, :], hf[half][:],
                                  h_hi[u.par][:, 2 * half:2 * half + 2, :].bitcast(f32),
                                  ALU.subtract).then_inc(h_lo_done, 1)

            def unit(u, e, e_before, wp, wp_before, spare):
                indices(u.ahead(2))
                for half in range(2):
                    n = 2 * u.t + half
                    ve.wait_ge(tanh_done, n + 1)
                    gate = b_gate[half][:, 0, :].rearrange("p (m n) -> p m n", m=2)
                    dve.scalar_tensor_tensor(sg[half][:], th[half][:], 1.0, gate, ALU.add, ALU.mult).then_inc(sg_done, 1)
                    ve.wait_ge(up_ps, n + 1)
                    ve.wait_ge(sg_done, n + 1)
                    if not u.first(1):
                        ve.wait_ge(h_lo_done, n - 1)
                    up = b_up[half][:, 0, :].rearrange("p (m n) -> p m n", m=2)
                    dve.tensor_tensor(hf[half][:], sg[half][:], up, ALU.mult).then_inc(hf_done, 1)
                    if spare:
                        meanwhile(e, wp, u.par, half)
                    if half == 0:
                        rest_rows(u.ahead(1))
                        rest_inner(u, 0)
                if not u.first(1):
                    weigh(u.back(1), e_before)
                rest_inner(u, 1)
                row_weights(u.ahead(1))

            def first_list(e):
                low_factors(e, e)
                tile_places(e, e)
                numbers_there(e, e)
                ve.wait_ge(ab_done, e + 1)
                dve.tensor_tensor(*low_product(e, LOW_V, TILES), ALU.mult).then_inc(low_v, 1)

            first_list(0)
            fill_list(0, 0, 0)
            indices(Unit(0, 0))
            indices(Unit(0, 1))
            first_list(1)
            rest_rows(Unit(0, 0))
            row_weights(Unit(0, 0))
            fill_list(1, 1, in_front(ve, 1))

            def meanwhile(e, par_e, par, half):
                if par == 0 and half == 0:
                    tile_places(e + 2, par_e)
                elif par == 0:
                    numbers_there(e + 2, par_e)
                else:
                    rest_weights(ve, e + 1, 1 - par_e, (half,))

            def between(e, par_e, when, front):
                if when == 0:
                    low_factors(e + 2, par_e)
                if when == 2:
                    fill_list(e + 2, par_e, in_front(ve, e + 2))

            total = run_experts(ve, unit, between)
            weigh(Unit(total, 0).back(1), EXPERTS - 1)

        @block.tensor
        def _(pe):
            pe.wait_ge(const_in, 8 * 16)

            def probs_t(tile, half):
                t, p = tile.t, tile.par
                if half == 0:
                    pe.wait_ge(pn_done, t + 1)
                if not (isinstance(t, int) and t == 0 and half == 0):
                    pe.wait_ge(pt_done, 2 * t + half)
                for j in range(PAIRS // 2):
                    pair = half * (PAIRS // 2) + j
                    l = te.transpose(b_pt[:, 0, j * P:(j + 1) * P],
                                     pr[p][:, 2 * pair:2 * pair + 2, :].rearrange("p h k -> p (h k)"), ident_s[:])
                l.then_inc(pt_ps, 1)

            def probs_t_first(tile):
                probs_t(tile, 0)

            def probs_t_second(tile):
                probs_t(tile, 1)

            def project(tile):
                t, p = tile.t, tile.par
                pe.wait_ge(ctxt_done, 2 * t + 2)
                for g in range(KD):
                    te.matmul(b_c[:, 0, D:2 * D], ctxt[p][:, g, :], wo_s[:, g, :], start=(g == 0), stop=False)
                te.matmul(b_c[:, 0, D:2 * D], rmask[:], bias_r[:, 2, :], start=False, stop=True).then_inc(o_ps, 1)

            def scores(tile):
                t, p = tile.t, tile.par
                pe.wait_ge(kbd_done, t + 1)
                before_tile(pe, sub_done, t, ago=1)
                for g in range(KD):
                    for b in range(BPT):
                        rows = slice(b * SEQ, (b + 1) * SEQ)
                        l = te.matmul(b_s[rows, g, :], qt[p][:, g, rows],
                                      kbd[p][:, b, g].rearrange("p h k -> p (h k)"), start=True, stop=True)
                l.then_inc(s_ps, 1)

            def keys_queries(tile):
                t, p = tile.t, tile.par
                if isinstance(t, int) and t == 0:
                    pe.wait_ge(prep, PREP_ALL)
                pe.wait_ge(ctx_in[p], (tile.i + 1) * 64)
                before_tile(pe, qkn_done, t, ago=1)
                keys = b_qk[:, 0, D:2 * D]
                te.matmul(keys, cm[p][:, 1:1 + BPT, :].rearrange("p b k -> p (b k)"), wkm_s[:, 0:D], start=True, stop=False)
                te.matmul(keys, cd[p][:, 1:1 + BPT, :].rearrange("p b k -> p (b k)"), wkd_s[:, 0:D], start=False, stop=False)
                te.matmul(keys, rmask[:], bias_r[:, 1, :], start=False, stop=True)
                pe.wait_ge(xnt_done, t + 1)
                for k in range(KD):
                    te.matmul(b_qk[:, 0, 0:D], xnt[p][:, k, :], wq_s[:, k, :], start=(k == 0), stop=False)
                te.matmul(b_qk[:, 0, 0:D], rmask[:], bias_r[:, 0, :], start=False, stop=True).then_inc(qk_ps, 1)

            def transpose_heads(tile):
                t, p = tile.t, tile.par
                pe.wait_ge(qkn_done, t + 1)
                before_tile(pe, qkt_done, t, ago=1)
                for k in range(2 * KD):
                    l = te.transpose(b_qkt[:, 0, k * P:(k + 1) * P], qkn[p][:, k * P:(k + 1) * P], ident_s[:])
                l.then_inc(qkt_ps, 1)

            def transpose_x(tile):
                t, p = tile.t, tile.par
                pe.wait_ge(xn_done, t + 1)
                before_tile(pe, xnt_done, t, ago=1)
                before_tile(pe, lg_done, t, ago=STAGES)
                for k in range(KD):
                    l = te.transpose(b_x[:, 0, k * P:(k + 1) * P], xn[p][:, k * P:(k + 1) * P], ident_s[:])
                l.then_inc(xnt_ps, 1)

            def values(tile):
                t, p = tile.t, tile.par
                before_tile(pe, vbd_done, t, ago=1)
                for b in range(BPT):
                    vals = b_v[:, 0, b * D:(b + 1) * D]
                    te.matmul(vals, cm[p][:, 2 * b:2 * b + 2, :].rearrange("p b k -> p (b k)"), wkm_s[:, D:2 * D],
                              start=True, stop=False)
                    l = te.matmul(vals, cd[p][:, 2 * b:2 * b + 2, :].rearrange("p b k -> p (b k)"), wkd_s[:, D:2 * D],
                                  start=False, stop=True)
                l.then_inc(v_ps, 1)

            def transpose_x1(tile):
                t, p = tile.t, tile.par
                pe.wait_ge(x1n_done, t + 1)
                before_tile(pe, lg_done, t, ago=1)
                if not isinstance(t, int) or t + STAGES <= TILES:
                    pe.wait_ge(xnt_done, t + STAGES)
                for k in range(KD):
                    l = te.transpose(b_x[:, 0, k * P:(k + 1) * P], x1n[p][:, k * P:(k + 1) * P], ident_s[:])
                l.then_inc(x1nt_ps, 1)

            def attend(tile):
                t, p = tile.t, tile.par
                pe.wait_ge(pt_done, 2 * t + 2)
                pe.wait_ge(vbd_done, t + 1)
                before_tile(pe, ctxt_done, t, per=2, ago=1)
                before_tile(pe, x1_done, t, ago=1)
                for pair in range(PAIRS):
                    g, row = divmod(pair * 2 * HD, P)
                    for b in range(BPT):
                        l = te.matmul(b_c[row:row + 2 * HD, 0, g * P + b * SEQ:g * P + (b + 1) * SEQ],
                                      vbd[p][:, b, pair * 2 * HD:(pair + 1) * 2 * HD],
                                      pt[p][:, pair, b * SEQ:(b + 1) * SEQ], start=True, stop=True)
                l.then_inc(c_ps, 1)

            def route_logits(tile):
                t, p = tile.t, tile.par
                pe.wait_ge(x1nt_done, t + 1)
                for k in range(KD):
                    l = te.matmul(b_x[:, 0, D:D + EXPERTS], x1nt[p][:, k, :], rt_s[:, k, :],
                                  start=(k == 0), stop=(k == KD - 1))
                l.then_inc(lg_ps, 1)

            run_tiles(pe, [(5, project), (3, scores), (1, keys_queries), (2, transpose_heads), (4, probs_t_first),
                      (0, transpose_x), (4, probs_t_second), (2, values), (5, transpose_x1), (4, attend), (5,
                      route_logits)])

            pe.wait_ge(route, KEPT_STEP)
            for k in range(2):
                l = te.matmul(b_rank[:, 0, k * EXPERTS * TILES:(k + 1) * EXPERTS * TILES], lower_s[:, k, :],
                              kept[:].rearrange("p e t -> p (e t)"), start=True, stop=True)
            l.then_inc(rank_ps, 1)

            def make_list(e, par):
                if isinstance(e, int) and e < 2:
                    pe.wait_ge(low_g, e + 1)
                    pe.wait_ge(low_v, e + 1)
                else:
                    pe.wait_ge(low_g, 2 * e)
                pe.wait_ge(high_v, 2 * e + 2)
                if not isinstance(e, int) or e:
                    pe.wait_ge(listed_done, e)
                for t in range(TILES):
                    l = te.matmul(b_list[:, 0, par * 2 * TILES:(par + 1) * 2 * TILES], in_low[par][:, t, :],
                                  in_high[par][:, t].rearrange("p c t -> p (c t)"), start=(t == 0), stop=(t == TILES - 1))
                l.then_inc(list_ps, 1)

            make_list(0, 0)

            def transpose_rows(u):
                pe.wait_ge(gathered[u.par], UT * 16 * (u.i + 1))
                if not u.first(1):
                    pe.wait_ge(xl_done, u.t)
                for k in range(KD):
                    for s in range(UT):
                        l = te.transpose(b_xt[:, 0, k * UNIT + s * P:k * UNIT + (s + 1) * P],
                                         gat[u.par][:, s, k * P:(k + 1) * P], ident_s[:])
                l.then_inc(xt_ps, 1)

            def gate_up(u, wp, half):
                pe.wait_ge(xl_done, u.t + 1)
                for which, b, sm_ in ((0, b_gate[half], gate_ps), (1, b_up[half], up_ps)):
                    if not u.first(1):
                        pe.wait_ge(hf_done, 2 * u.t + half - 1)
                    for mm in range(2):
                        m = 2 * half + mm
                        first = True
                        for k in range(KD):
                            o = which * WPART + k * INNER + m * P
                            for w, xs in ((w_hi, xh), (w_hi, xl), (w_lo, xh)):
                                l = te.matmul(b[:, 0, mm * UNIT:(mm + 1) * UNIT], w[wp][:, o:o + P],
                                              xs[u.par][:, k, :], start=first, stop=(k == KD - 1 and w is w_lo))
                                first = False
                    l.then_inc(sm_, 1)

            def down(u, wp):
                pe.wait_ge(h_lo_done, 2 * u.t + 2)
                if not u.first(1):
                    pe.wait_ge(y_done, u.t)
                for s in range(UT):
                    first = True
                    for k in range(MT):
                        o = 2 * WPART + k * D
                        for h, w in ((h_hi, w_hi), (h_hi, w_lo), (h_lo, w_hi)):
                            l = te.matmul(b_down[u.par][:, 0, s * D:(s + 1) * D], h[u.par][:, k, s * P:(s + 1) * P],
                                          w[wp][:, o:o + D], start=first, stop=(k == MT - 1 and h is h_lo))
                            first = False
                l.then_inc(down_ps, 1)

            def unit(u, e, e_before, wp, wp_before, spare):
                pe.wait_ge(w_lo_done, 3 * (e + 1))
                gate_up(u, wp, 0)
                transpose_rows(u.ahead(1))
                gate_up(u, wp, 1)
                if not u.first(1):
                    down(u.back(1), wp_before)

            transpose_rows(Unit(0, 0))
            make_list(1, 1)

            def between(e, par_e, when, front):
                if when == 2:
                    make_list(e + 2, par_e)

            total = run_experts(pe, unit, between)
            down(Unit(total, 0).back(1), 1)


def kernel(**inputs):
    import numpy as np
    import concourse.bacc as bacc
    from concourse import mybir as mb
    from concourse.bass_utils import run_bass_kernel_spmd

    a = {k.removeprefix("L0_").removeprefix("xattn_").removeprefix("ffn_"): np.asarray(v) for k, v in inputs.items()}

    def by_rows(w):
        return w.reshape(-1, P, w.shape[-1]).transpose(1, 0, 2)

    both = np.concatenate([a["Wk"], a["Wv"]], axis=1).reshape(CD, HEADS, 2, HD).transpose(0, 2, 1, 3)
    both_b = np.concatenate([a["bk"], a["bv"]]).reshape(HEADS, 2, HD).transpose(1, 0, 2).reshape(2, D)
    dca_b = a["bkv_dca"].reshape(2, D)
    main = (np.arange(P) % KEYS < KEYS_MAIN).astype(np.float32)
    experts = [w.transpose(0, 2, 1).reshape(EXPERTS, KD, P, INNER).transpose(0, 2, 1, 3).reshape(EXPERTS, P, -1)
               for w in (a["gate_w"], a["up_w"])]
    experts.append(a["down_w"].transpose(0, 2, 1).reshape(EXPERTS, MT, P, D).transpose(0, 2, 1, 3).reshape(EXPERTS, P, -1))
    e, p, tile = np.arange(EXPERTS), np.arange(P)[:, None], np.arange(TILES)[None, :]

    def spread(v):
        return np.broadcast_to(v, (P, v.shape[1]))

    arrays = {
        "x": a["x"].reshape(TOKENS, D),
        "ctx_t": a["ctx_1024"].reshape(BATCH * KEYS, CD).T,
        "wq": by_rows(a["Wq"]),
        "wkv_main": both.reshape(CD, 2 * D),
        "wkv_dca": a["Wkv_dca"],
        "wo": by_rows(a["Wo"]),
        "router": by_rows(a["router_w"].T),
        "w_ffn": np.concatenate(experts, axis=2),
        "ln_scales": np.stack([np.tile(a[n], HG) for n in ("qn_w", "qn_b", "kn_w", "kn_b", "kn_dca_w", "kn_dca_b")], axis=1),
        "q_bias": np.stack([a["bq"]] * 4),
        "k_bias": np.stack([both_b[0], dca_b[0]] * 2),
        "o_bias": np.stack([a["bo"]] * 4),
        "v_bias": np.stack([both_b[1].reshape(KD, P).T, dca_b[1].reshape(KD, P).T], axis=1),
        "ident": np.eye(P, dtype=np.float32),
        "head_mask": (np.arange(P)[:, None] // HD == np.arange(HG)).astype(np.float32),
        "pair_mask": (np.arange(P)[:, None] // KEYS == np.arange(D) // HD % 2).astype(np.float32),
        "row_mask": np.stack([main, 1 - main] * 2),
        "hi_lo_rows": np.array(HI_LO, np.float32),
        "before": np.broadcast_to((e[None, :] < np.arange(EXPERTS + 1)[:, None]).astype(np.float32),
                                  (P, EXPERTS + 1, EXPERTS)),
        "lower": np.stack([(p < p.T), np.ones((P, P))], axis=1).astype(np.float32),
        "steps": np.concatenate([spread(p.T), spread(1 + tile), P * tile + p - MID,
                                 spread(BLOCK * (1 + tile)), TOKENS + p, MID - TOKENS - p],
                                axis=1).astype(np.float32),
    }
    nc = bacc.Bacc("TRN2", target_bir_lowering=False, num_devices=1)
    arrays = {n: np.ascontiguousarray(v) for n, v in arrays.items()}
    args = [nc.dram_tensor(n, v.shape, mb.dt.from_np(v.dtype), kind="ExternalInput").ap() for n, v in arrays.items()]
    args.append(nc.dram_tensor("out", (TOKENS + P, D), mb.dt.float32, kind="ExternalOutput").ap())
    args.append(nc.dram_tensor("rows", (TOKENS + P, ROW), mb.dt.float32, kind="Internal").ap())
    xattn_ffn_kernel(nc, *args)
    r = run_bass_kernel_spmd(nc, [arrays], core_ids=[0])
    return r.results[0]["out"][:TOKENS].reshape(BATCH, SEQ, D)
```
